# Optimizing a Trainium2 kernel written in Bass

```python
import numpy as np
import jax
import jax.numpy as jnp

def _softmax(x, axis=-1):
    return jax.nn.softmax(x, axis=axis)

def _gelu(x):
    return jax.nn.gelu(x, approximate=True)

def _silu(x):
    return jax.nn.silu(x)

def _sigmoid(x):
    return jax.nn.sigmoid(x)

def _layernorm(x, axis=-1, eps=1e-05):
    m = jnp.mean(x, axis=axis, keepdims=True)
    v = jnp.var(x, axis=axis, keepdims=True)
    return (x - m) / jnp.sqrt(v + eps)

def _scatter_add(tgt, idx, src, axis=0):
    return tgt.at[idx].add(src)

def _segment_sum(src, seg, n):
    return jax.ops.segment_sum(src, seg, n)
kernel_name = 'mk_sandwich_d1_jaxref_r4_e309be'

def setup_inputs(seed: int=0):
    np.random.seed(seed)
    _w = jnp.asarray

    def _L0_attn_setup():
        import jax, jax.numpy as jnp
        import numpy as np
        D_MODEL = 256
        SCALE = float(np.sqrt(D_MODEL))
        key = jax.random.key(seed)
        k1, k2, k3 = jax.random.split(key, 3)
        input_data = jax.random.normal(k1, (4, 512, D_MODEL), dtype=jnp.float32)
        qk = jax.random.normal(k2, (D_MODEL, D_MODEL), dtype=jnp.float32) / SCALE
        ov = jax.random.normal(k3, (D_MODEL, D_MODEL), dtype=jnp.float32) / SCALE
        return {'input_data': input_data, 'qk': qk, 'ov': ov}
    _L0_attn_in = _L0_attn_setup()

    def _L0_ffn_setup():
        import jax, jax.numpy as jnp
        import numpy as np
        D_IN, D_HID = (256, 1024)

        def _ternary(key, shape):
            return jax.random.randint(key, shape, -1, 2).astype(jnp.float32)

        def _tlin(x, w, s):
            return jnp.einsum('bsi,oi->bso', x, w) * s
        key = jax.random.key(seed)
        ks = jax.random.split(key, 12)
        inv = lambda fan: 1.0 / np.sqrt(fan).astype(np.float32)
        return {'x': jax.random.normal(ks[0], (4, 512, D_IN), dtype=jnp.float32), 'w1_w': _ternary(ks[1], (D_HID, D_IN)), 'w1_s': jax.random.uniform(ks[2], (D_HID,), dtype=jnp.float32) * inv(D_IN), 'w2_w': _ternary(ks[3], (D_HID, D_IN)), 'w2_s': jax.random.uniform(ks[4], (D_HID,), dtype=jnp.float32) * inv(D_IN), 'h1_w': _ternary(ks[5], (D_HID, D_HID)), 'h1_s': jax.random.uniform(ks[6], (D_HID,), dtype=jnp.float32) * inv(D_HID), 'h2_w': _ternary(ks[7], (D_HID, D_HID)), 'h2_s': jax.random.uniform(ks[8], (D_HID,), dtype=jnp.float32) * inv(D_HID), 'w3_w': _ternary(ks[9], (D_IN, D_HID)), 'w3_s': jax.random.uniform(ks[10], (D_IN,), dtype=jnp.float32) * inv(D_HID)}
    _L0_ffn_in = _L0_ffn_setup()
    _d = {'L0_attn_input_data': _L0_attn_in['input_data'], 'L0_attn_qk': _L0_attn_in['qk'], 'L0_attn_ov': _L0_attn_in['ov'], 'L0_ffn_w1_w': _L0_ffn_in['w1_w'], 'L0_ffn_w1_s': _L0_ffn_in['w1_s'], 'L0_ffn_w2_w': _L0_ffn_in['w2_w'], 'L0_ffn_w2_s': _L0_ffn_in['w2_s'], 'L0_ffn_h1_w': _L0_ffn_in['h1_w'], 'L0_ffn_h1_s': _L0_ffn_in['h1_s'], 'L0_ffn_h2_w': _L0_ffn_in['h2_w'], 'L0_ffn_h2_s': _L0_ffn_in['h2_s'], 'L0_ffn_w3_w': _L0_ffn_in['w3_w'], 'L0_ffn_w3_s': _L0_ffn_in['w3_s']}
    _x0 = _d['L0_attn_input_data']
    _d['L0_attn_input_data'] = jax.random.normal(jax.random.fold_in(jax.random.key(seed), 1), (8, 512, 256), dtype=_x0.dtype)
    del _x0
    return _d

def reference(L0_attn_input_data, L0_attn_qk, L0_attn_ov, L0_ffn_w1_w, L0_ffn_w1_s, L0_ffn_w2_w, L0_ffn_w2_s, L0_ffn_h1_w, L0_ffn_h1_s, L0_ffn_h2_w, L0_ffn_h2_s, L0_ffn_w3_w, L0_ffn_w3_s):

    def _L0_attn_ref(input_data, qk, ov):
        import jax, jax.numpy as jnp
        import numpy as np
        D_MODEL = 256
        SCALE = float(np.sqrt(D_MODEL))
        S = input_data.shape[1]
        scores = jnp.einsum('bsd,de,bte->bst', input_data, qk, input_data) / SCALE
        causal = jnp.tril(jnp.ones((S, S), dtype=bool))
        scores = jnp.where(causal, scores, -jnp.inf)
        attn = jax.nn.softmax(scores, axis=-1)
        return jnp.einsum('bst,btd,de->bse', attn, input_data, ov)

    def _L0_ffn_ref(x, w1_w, w1_s, w2_w, w2_s, h1_w, h1_s, h2_w, h2_s, w3_w, w3_s):
        import jax, jax.numpy as jnp
        import numpy as np
        D_IN, D_HID = (256, 1024)

        def _ternary(key, shape):
            return jax.random.randint(key, shape, -1, 2).astype(jnp.float32)

        def _tlin(x, w, s):
            return jnp.einsum('bsi,oi->bso', x, w) * s
        h = jax.nn.silu(_tlin(x, w1_w, w1_s)) * _tlin(x, w2_w, w2_s)
        h = jax.nn.gelu(_tlin(h, h1_w, h1_s), approximate=False)
        h = jax.nn.gelu(_tlin(h, h2_w, h2_s), approximate=False)
        return _tlin(h, w3_w, w3_s)
    x = L0_attn_input_data
    x = x + _layernorm(_L0_attn_ref(_layernorm(x, axis=-1), L0_attn_qk, L0_attn_ov), axis=-1)
    x = x + _layernorm(_L0_ffn_ref(_layernorm(x, axis=-1), L0_ffn_w1_w, L0_ffn_w1_s, L0_ffn_w2_w, L0_ffn_w2_s, L0_ffn_h1_w, L0_ffn_h1_s, L0_ffn_h2_w, L0_ffn_h2_s, L0_ffn_w3_w, L0_ffn_w3_s), axis=-1)
    return x

_drawn_inputs = setup_inputs


def setup_inputs(seed=0):
    import zlib

    import numpy as np

    out = dict(_drawn_inputs(seed))
    spreads = {}
    factors = {}
    for name, (base, spread) in spreads.items():
        noise = np.random.default_rng([zlib.crc32(name.encode()), seed]).standard_normal(out[name].shape)
        drawn = base * np.exp(spread * noise) if base else spread * noise
        out[name] = jnp.asarray(drawn.astype(out[name].dtype))
    for name, factor in factors.items():
        out[name] = (out[name] * factor).astype(out[name].dtype)
    return out
```

```python
import concourse.bass as bass
from concourse import mybir
from contextlib import ExitStack

P = 128


def sandwich_kernel(nc, x_in, qk_in, ov_in, w1_in, w2_in, h1_in, h2_in, w3_in,
                    scales_in, w3_scale_in, out):
    fp32, fp32r = mybir.dt.float32, mybir.dt.float32r
    fp16, i32 = mybir.dt.float16, mybir.dt.int32
    ALU, ACT, AX = mybir.AluOpType, mybir.ActivationFunctionType, mybir.AxisListType

    CHUNKS, S, D = x_in.shape
    HID = w1_in.shape[1] // (D // P)
    TT = S // P
    DT = D // P
    HT = HID // P
    EPS = 1e-5
    SCORE_SCALE = float(D) ** -0.5
    MASKED = -3.0e38
    BANK = 512

    TRI = [7 * P, 2 * P, 4 * P, 0]

    at = [(nc.sbuf_base + 63) // 64 * 64]

    def place(name, cols, dtype=fp32, over=None):
        offset = at[0] if over is None else over
        t = nc.alloc_sbuf_tensor_at(name, [P, cols], dtype, offset=offset)
        if over is None:
            at[0] += (cols * 4 + 31) // 32 * 32
            assert at[0] <= nc.sbuf_usable_end
        return t, offset

    W_PARTS = [("w1", w1_in), ("w2", w2_in), ("h1", h1_in), ("h2", h2_in), ("w3", w3_in)]
    W_COLS = sum(src.shape[1] for _, src in W_PARTS)
    w = place("w", W_COLS, fp32r)[0]
    w_first = {}
    for name, _ in W_PARTS:
        w_first[name] = sum(src.shape[1] for _, src in W_PARTS[:len(w_first)])
    PIECE = 2048
    SLOTS = 4 * HT * S // PIECE
    pieces = [(n, src, c) for n, src in W_PARTS for c in range(0, src.shape[1], PIECE)]
    LAYERS = [("w1", "w2"), ("h1",), ("h2",), ("w3",)]

    dense_hi = place("dense_hi", 2 * DT * D, fp32r)[0]
    dense_lo = place("dense_lo", 2 * DT * D, fp32r)[0]
    stage = place("stage", SLOTS * PIECE, over=at[0])[0]
    hid_hi = [place(f"hid{n}_hi", HT * S, fp32r)[0] for n in range(2)]
    hid_lo = [place(f"hid{n}_lo", HT * S, fp32r)[0] for n in range(2)]
    hid_new = place("hid_new", 2 * S)[0]
    x_tok = place("x_tok", TT * D)[0]
    resid = place("resid", TT * D)[0]
    y_tok, y_at = place("y_tok", TT * D)
    n_tok, n_at = place("n_tok", TT * D)
    probs = place("probs", TT * D, over=n_at)[0]
    xT_hi, xT_hi_at = place("xT_hi", DT * S, fp32r)
    xT_lo, xT_lo_at = place("xT_lo", DT * S, fp32r)
    pT_hi = place("pT_hi", DT * S, fp32r, over=xT_hi_at)[0]
    pT_lo = place("pT_lo", DT * S, fp32r, over=xT_lo_at)[0]
    qT_hi, qT_hi_at = place("qT_hi", DT * S, fp32r)
    qT_lo, qT_lo_at = place("qT_lo", DT * S, fp32r)
    fT_hi = place("fT_hi", DT * S, fp32r, over=qT_hi_at)[0]
    fT_lo = place("fT_lo", DT * S, fp32r, over=qT_lo_at)[0]
    v_hi = place("v_hi", TT * D, fp32r)[0]
    v_lo = place("v_lo", TT * D, fp32r)[0]
    dense_raw = place("dense_raw", 2 * DT * D, over=y_at)[0]

    ident = place("ident", P)[0]
    causal = place("causal", P)[0]
    w3_scale = place("w3_scale", D)[0]
    scales = place("scales", 4 * HT)[0]
    ones = place("ones", 1)[0]
    wait_here = place("wait_here", 2)[0]
    first_counts = place("first_counts", 2)[0]
    neg_half = place("neg_half", TT)[0]
    row_max = place("row_max", TT)[0]
    row_sum = place("row_sum", TT)[0]
    sum_eps = place("sum_eps", TT)[0]
    low_squares = place("low_squares", len(LAYERS) * P, over=n_at)[0]
    low_sum = place("low_sum", len(LAYERS))[0]
    low_flag = place("low_flag", len(LAYERS))[0]
    NORMS = ["x", "att", "mid", "out"]
    stats, moments, var_eps, rstd = {}, {}, {}, {}
    for n in NORMS:
        stats[n] = place(f"{n}_stats", TT * 6)[0]
        moments[n] = place(f"{n}_moments", TT * 2)[0]
        var_eps[n] = place(f"{n}_var_eps", TT)[0]
        rstd[n] = place(f"{n}_rstd", TT)[0]

    def w_tile(name, k, first, cols):
        c = w_first[name] + k * (D if name == "w3" else HID) + first
        return w[:, c:c + cols]

    def low_halves(piece, c):
        first = (piece % SLOTS) * PIECE + c * P
        return stage[:, first:first + P].bitcast(fp16).rearrange("p (n two) -> p n two", two=2)[:, :, 0]

    def col(t, i, n=BANK):
        return t[:, i * n:(i + 1) * n]

    ctx = ExitStack()
    with ctx:
        main = [ctx.enter_context(nc.psum_tensor(f"main{i}", [P, BANK], fp32)) for i in range(4)]
        side = [ctx.enter_context(nc.psum_tensor(f"side{i}", [P, BANK], fp32)) for i in range(4)]

        def sem(name):
            return ctx.enter_context(nc.semaphore(name))

        x_loaded, out_stored = sem("x_loaded"), sem("out_stored")
        dense_loaded, scales_loaded = sem("dense_loaded"), sem("scales_loaded")
        piece_loaded = [sem(f"piece_loaded{i}") for i in range(SLOTS)]
        w_tile_loaded = [sem(f"w_tile{g}_loaded") for g in range(len(LAYERS))]
        const_set, dense_hi_set, dense_lo_set = sem("const_set"), sem("dense_hi_set"), sem("dense_lo_set")
        piece_rounded, piece_squared = sem("piece_rounded"), sem("piece_squared")
        low_squares_set, low_sum_set, low_sum_psum, low_flag_set = (
            sem("low_squares_set"), sem("low_sum_set"), sem("low_sum_psum"), sem("low_flag_set"))
        stats_set = {n: sem(f"{n}_stats_set") for n in NORMS}
        moments_set = {n: sem(f"{n}_moments_set") for n in NORMS}
        var_eps_set = {n: sem(f"{n}_var_eps_set") for n in NORMS}
        rstd_set = {n: sem(f"{n}_rstd_set") for n in NORMS}
        sum_eps_set = sem("sum_eps_set")
        normed = {n: sem(f"{n}_normed") for n in NORMS}
        xT_psum, xT_hi_set, xT_lo_set = sem("xT_psum"), sem("xT_hi_set"), sem("xT_lo_set")
        q_psum, q_hi_set, q_lo_set = sem("q_psum"), sem("q_hi_set"), sem("q_lo_set")
        v_psum, v_hi_set, v_lo_set = sem("v_psum"), sem("v_hi_set"), sem("v_lo_set")
        scores_psum, masked, max_set, probs_set = (
            sem("scores_psum"), sem("masked"), sem("max_set"), sem("probs_set"))
        pT_psum, pT_hi_set, pT_lo_set = sem("pT_psum"), sem("pT_hi_set"), sem("pT_lo_set")
        att_psum = sem("att_psum")
        x_updated, resid_kept = sem("x_updated"), sem("resid_kept")
        fT_psum, fT_hi_set, fT_lo_set = sem("fT_psum"), sem("fT_hi_set"), sem("fT_lo_set")
        gate_psum, lin_psum, gate_read, lin_read = (
            sem("gate_psum"), sem("lin_psum"), sem("gate_read"), sem("lin_read"))
        hid_psum = [None, sem("hid1_psum"), sem("hid2_psum")]
        gelu_set = [None, sem("gelu1_set"), sem("gelu2_set")]
        hi_set = [sem(f"hid{n}_hi_set") for n in range(3)]
        lo_set = [sem(f"hid{n}_lo_set") for n in range(3)]
        ff_psum, ff_read = sem("ff_psum"), sem("ff_read")
        w3_half_used = sem("w3_half_used")
        out_set = sem("out_set")

        block = ctx.enter_context(nc.Block())

        def run(eng, body):
            body(None, 0)
            with eng.Fori(0, CHUNKS - 1) as i:
                body(i, i + 1)
            body(CHUNKS - 1, None)

        @block.sync
        def _(sp):
            def load_x(a):
                if not isinstance(a, int):
                    sp.wait_ge(resid_kept, a)
                sp.dma_start(x_tok[:, :].rearrange("p (j d) -> p j d", j=TT),
                             x_in[a, :, :].rearrange("(j p) d -> p j d", p=P)).then_inc(x_loaded, 16)

            def store(f):
                sp.wait_ge(out_set, TT * f + TT)
                sp.dma_start(out[f, :, :].rearrange("(j p) d -> p j d", p=P),
                             y_tok[:, :].rearrange("p (j d) -> p j d", j=TT)).then_inc(out_stored, 16)

            load_x(0)
            sp.dma_start(dense_raw[:, 0:DT * D], qk_in).then_inc(dense_loaded, 16)
            sp.dma_start(dense_raw[:, DT * D:2 * DT * D], ov_in).then_inc(dense_loaded, 16)
            sp.dma_start(scales[:, :], scales_in).then_inc(scales_loaded, 16)
            sp.dma_start(w3_scale[:, :], w3_scale_in.partition_broadcast(P)).then_inc(scales_loaded, 16)
            for n, (_, src, c) in enumerate(pieces):
                if n >= SLOTS:
                    sp.wait_ge(piece_rounded, n - SLOTS + 1)
                    sp.wait_ge(piece_squared, n - SLOTS + 1)
                slot = (n % SLOTS) * PIECE
                sp.dma_start(stage[:, slot:slot + PIECE], src[:, c:c + PIECE]).then_inc(piece_loaded[n % SLOTS], 16)

            flags = [sp.alloc_register(f"sp_low_{g}") for g in range(len(LAYERS))]
            sp.wait_ge(low_flag_set, 1)
            for g, reg in enumerate(flags):
                sp.reg_load(reg, low_flag[0:1, g:g + 1].bitcast(i32))

            def weight_tiles(f):
                psums = [lin_psum, hid_psum[1], hid_psum[2]]
                for g in range(len(LAYERS)):
                    with sp.If_ne(flags[g], 0):
                        sp.wait_ge(out_stored, 16 * f + 16)
                        for n in range(HT):
                            if n == 0:
                                if g > 0:
                                    sp.wait_ge(psums[g - 1], HT * f + HT)
                            elif g < 3:
                                sp.wait_ge(psums[g], HT * f + n)
                            elif n % 4 == 0:
                                sp.wait_ge(ff_psum, 2 * f + n // 4)
                            else:
                                sp.wait_ge(w3_half_used, (2 * TT - 2) * f + n - n // 4)
                            if g == 0:
                                for part, src in enumerate((w1_in, w2_in)):
                                    sp.dma_start(
                                        y_tok[:, part * DT * P:(part + 1) * DT * P].rearrange(
                                            "p (k o) -> p k o", k=DT),
                                        src.rearrange("p (k o) -> p k o", k=DT)[:, :, n * P:(n + 1) * P]
                                    ).then_inc(w_tile_loaded[g], 16)
                            elif g < 3:
                                sp.dma_start(
                                    y_tok[:, :].rearrange("p (k o) -> p k o", k=HT),
                                    (h1_in, h2_in)[g - 1].rearrange("p (k o) -> p k o", k=HT)[
                                        :, :, n * P:(n + 1) * P]).then_inc(w_tile_loaded[g], 16)
                            else:
                                half = HT // 2 * D
                                sp.dma_start(y_tok[:, 0:half], w3_in[:, n % 2 * half:(n % 2 + 1) * half]
                                             ).then_inc(w_tile_loaded[g], 16)

            with sp.Fori(0, CHUNKS - 1) as i:
                load_x(i + 1)
                weight_tiles(i)
                store(i)
            weight_tiles(CHUNKS - 1)
            store(CHUNKS - 1)
            sp.wait_ge(out_stored, 16 * CHUNKS + 16)

        @block.gpsimd
        def _(pool):
            pool.memset(ident[:, :], 0.0).then_inc(const_set, 1)
            pool.memset(causal[:, :], 0.0).then_inc(const_set, 1)
            pool.memset(ones[:, :], 1.0).then_inc(const_set, 1)
            pool.memset(neg_half[:, :], -0.5).then_inc(const_set, 1)
            pool.memset(wait_here[:, :], 0.0).then_inc(const_set, 1)
            pool.memset(first_counts[:, 0:1], 0.0).then_inc(out_stored, 16)
            pool.memset(first_counts[:, 1:2], 0.0).then_inc(ff_read, TT)
            pool.wait_ge(const_set, 5)
            pool.affine_select(out=ident[:, :], in_=ident[:, :], compare_op=ALU.not_equal, fill=1.0,
                               base=0, pattern=[[-1, P]], channel_multiplier=1).then_inc(const_set, 1)
            pool.affine_select(out=causal[:, :], in_=causal[:, :], compare_op=ALU.is_ge, fill=MASKED,
                               base=0, pattern=[[-1, P]], channel_multiplier=1).then_inc(const_set, 1)

            def root(n, c):
                pool.wait_ge(var_eps_set[n], c + 1)
                pool.tensor_tensor(rstd[n][:, :], var_eps[n][:, :], neg_half[:, :],
                                   ALU.pow).then_inc(rstd_set[n], 1)

            def body(f, a):
                if a is not None:
                    root("x", a)
                    root("att", a)
                    root("mid", a)
                if f is not None:
                    root("out", f)

            def round_pieces(first, last):
                for n in range(first, last):
                    pool.wait_ge(piece_loaded[n % SLOTS], 16 * (n // SLOTS + 1))
                    name, _, c = pieces[n]
                    slot = (n % SLOTS) * PIECE
                    pool.tensor_copy(w[:, w_first[name] + c:w_first[name] + c + PIECE],
                                     stage[:, slot:slot + PIECE]).then_inc(piece_rounded, 1)

            root("x", 0)
            round_pieces(0, 4)
            root("att", 0)
            root("mid", 0)
            round_pieces(4, len(pieces))
            with pool.Fori(0, CHUNKS - 1) as i:
                body(i, i + 1)
            body(CHUNKS - 1, None)

        @block.scalar
        def _(act):
            def high(dst, src, ready, count, done, scale=1.0):
                act.wait_ge(ready, count)
                act.activation(dst, src, ACT.Copy, scale=scale).then_inc(done, 1)

            def first_layer(f, o):
                act.wait_ge(gate_psum, HT * f + o + 1)
                if o >= 2:
                    act.wait_ge(lo_set[0], HT * f + o - 1)
                act.activation(col(hid_new, o % 2), main[2 * (o % 2)][:, :], ACT.Silu,
                               scale=scales[:, o:o + 1]).then_inc(gate_read, 1)
                if o >= 1:
                    first_high(f, o - 1)

            def first_high(f, o):
                act.wait_ge(lin_read, HT * f + o + 1)
                act.activation(col(hid_hi[0], o), col(hid_new, o % 2), ACT.Copy).then_inc(hi_set[0], 1)

            def hidden(f, n, o):
                act.wait_ge(hid_psum[n], HT * f + o + 1)
                if o >= 2:
                    act.wait_ge(lo_set[n], HT * f + o - 1)
                else:
                    act.wait_ge(lo_set[n - 1], HT * f + HT - 1 + o)
                act.activation(col(hid_new, o % 2), main[o % 4][:, :], ACT.Gelu,
                               scale=scales[:, (n + 1) * HT + o:(n + 1) * HT + o + 1]
                               ).then_inc(gelu_set[n], 1)

            def softmax(a, j):
                act.wait_ge(max_set, TT * a + j + 1)
                if j == 3:
                    act.wait_ge(pT_psum, TT * a + 2)
                w = (j + 1) * P
                act.activation(probs[:, TRI[j]:TRI[j] + w], side[(j + 2) % 4][:, 0:w], ACT.Exp,
                               bias=row_max[:, j:j + 1], accum_out=row_sum[:, j:j + 1]
                               ).then_inc(probs_set, 1)

            def probs_high(a, j):
                if j == 3:
                    act.wait_ge(att_psum, 2 * a + 1)
                w = (j + 1) * P
                high(pT_hi[:, TRI[j]:TRI[j] + w], side[(j + 2) % 4][:, 0:w], pT_psum,
                     TT * a + j + 1, pT_hi_set)

            def body(f, a):
                if f is not None:
                    for o in range(HT):
                        first_layer(f, o)
                    first_high(f, HT - 1)
                if a is not None:
                    for k in range(DT):
                        high(col(xT_hi, k), side[k][:, :], xT_psum, DT * a + k + 1, xT_hi_set)
                if f is not None:
                    hidden(f, 1, 0)
                if a is not None:
                    for e in range(DT):
                        high(col(qT_hi, e), side[2 + e][:, :], q_psum, DT * a + e + 1, q_hi_set,
                             scale=SCORE_SCALE)
                if f is not None:
                    hidden(f, 1, 1)
                if a is not None:
                    for h in range(2):
                        high(col(v_hi, h), side[h][:, :], v_psum, 2 * a + h + 1, v_hi_set)
                if f is not None:
                    hidden(f, 1, 2)
                    hidden(f, 1, 3)
                if a is not None:
                    for j in range(3):
                        softmax(a, j)
                if f is not None:
                    hidden(f, 1, 4)
                if a is not None:
                    probs_high(a, 0)
                    probs_high(a, 1)
                    softmax(a, 3)
                if f is not None:
                    hidden(f, 1, 5)
                if a is not None:
                    probs_high(a, 2)
                if f is not None:
                    hidden(f, 1, 6)
                if a is not None:
                    probs_high(a, 3)
                if f is not None:
                    hidden(f, 1, 7)
                    for o in range(HT):
                        hidden(f, 2, o)
                if a is not None:
                    for k in range(DT):
                        high(col(fT_hi, k), side[k][:, :], fT_psum, DT * a + k + 1, fT_hi_set)

            act.wait_ge(dense_loaded, 32)
            act.activation(dense_hi[:, :], dense_raw[:, :], ACT.Copy).then_inc(dense_hi_set, 1)
            act.wait_ge(scales_loaded, 32)
            run(act, body)

        @block.vector
        def _(dve):
            def low(dst, src, hi, ready, count, done, scale=None):
                dve.wait_ge(ready, count)
                if scale is None:
                    ins = dve.tensor_tensor(dst, src, hi.bitcast(fp32), ALU.subtract)
                else:
                    ins = dve.scalar_tensor_tensor(dst, src, scale, hi.bitcast(fp32),
                                                   ALU.mult, ALU.subtract)
                ins.then_inc(done, 1)

            def norm_stats(n, c, j, src):
                dve.bn_stats(stats[n][:, 6 * j:6 * j + 6], src).then_inc(stats_set[n], 1)

            def norm_moments(n, c, tiles):
                dve.wait_ge(stats_set[n], TT * c + max(tiles) + 1)
                dve.tensor_copy(wait_here[0:1, 1:2], wait_here[0:1, 0:1])
                for j in tiles:
                    dve.bn_aggr(moments[n][:, 2 * j:2 * j + 2],
                                stats[n][:, 6 * j:6 * j + 6]).then_inc(moments_set[n], 1)

            def variances(n):
                return moments[n][:, :].rearrange("p (j m) -> p j m", m=2)[:, :, 1]

            def add_eps(n, c):
                dve.wait_ge(moments_set[n], TT * c + TT)
                dve.tensor_scalar(var_eps[n][:, :], variances(n), EPS, None,
                                  ALU.add).then_inc(var_eps_set[n], 1)

            def norm_apply(n, c, j, dst, src):
                if j == 0:
                    dve.wait_ge(rstd_set[n], c + 1)
                dve.tensor_scalar(dst, src, moments[n][:, 2 * j:2 * j + 1], rstd[n][:, j:j + 1],
                                  ALU.subtract, ALU.mult).then_inc(normed[n], 1)

            def norm_x_stats(a):
                dve.wait_ge(x_loaded, 16 * a + 16)
                for j in range(TT):
                    norm_stats("x", a, j, col(x_tok, j, D))
                norm_moments("x", a, range(TT))
                add_eps("x", a)

            def norm_x_apply(a):
                for j in range(TT):
                    norm_apply("x", a, j, col(n_tok, j, D), col(x_tok, j, D))

            def first_gated(f, o):
                dve.wait_ge(lin_psum, HT * f + o + 1)
                dve.wait_ge(gate_read, HT * f + o + 1)
                dve.scalar_tensor_tensor(col(hid_new, o % 2), main[2 * (o % 2) + 1][:, :],
                                         scales[:, HT + o:HT + o + 1], col(hid_new, o % 2),
                                         ALU.mult, ALU.mult).then_inc(lin_read, 1)

            def first_low(f, o):
                low(col(hid_lo[0], o), col(hid_new, o % 2), col(hid_hi[0], o), hi_set[0],
                    HT * f + o + 1, lo_set[0])

            def hidden(f, n, o):
                dve.wait_ge(gelu_set[n], HT * f + o + 1)
                dve.tensor_copy(col(hid_hi[n % 2], o), col(hid_new, o % 2)).then_inc(hi_set[n], 1)
                low(col(hid_lo[n % 2], o), col(hid_new, o % 2), col(hid_hi[n % 2], o), hi_set[n],
                    HT * f + o + 1, lo_set[n])

            def row_maxima(a, j):
                bank = side[(j + 2) % 4]
                dve.wait_ge(scores_psum, TT * a + j + 1)
                diag = bank[:, j * P:(j + 1) * P]
                dve.tensor_tensor(diag, diag, causal[:, :], ALU.add).then_inc(masked, 1)
                dve.wait_ge(masked, TT * a + j + 1)
                dve.tensor_reduce(row_max[:, j:j + 1], bank[:, 0:(j + 1) * P], AX.X, ALU.max,
                                  negate=True).then_inc(max_set, 1)

            def probs_low(a, j):
                w = (j + 1) * P
                low(pT_lo[:, TRI[j]:TRI[j] + w], side[(j + 2) % 4][:, 0:w],
                    pT_hi[:, TRI[j]:TRI[j] + w], pT_hi_set, TT * a + j + 1, pT_lo_set)

            def att_tile(j):
                return side[2 + j // 2][:, (j % 2) * D:(j % 2 + 1) * D]

            def norm_att_stats(a, h):
                dve.wait_ge(att_psum, 2 * a + h + 1)
                for j in (2 * h, 2 * h + 1):
                    norm_stats("att", a, j, att_tile(j))
                norm_moments("att", a, (2 * h, 2 * h + 1))

            def norm_att_root(a):
                dve.wait_ge(probs_set, TT * a + TT)
                dve.scalar_tensor_tensor(sum_eps[:, :], row_sum[:, :], EPS, row_sum[:, :],
                                         ALU.mult, ALU.mult).then_inc(sum_eps_set, 1)
                dve.wait_ge(sum_eps_set, a + 1)
                dve.wait_ge(moments_set["att"], TT * a + TT)
                dve.tensor_tensor(var_eps["att"][:, :], variances("att"), sum_eps[:, :],
                                  ALU.add).then_inc(var_eps_set["att"], 1)

            def update_x(a):
                for j in range(TT):
                    norm_apply("att", a, j, col(n_tok, j, D), att_tile(j))
                for j in range(TT):
                    dve.wait_ge(normed["att"], TT * a + j + 1)
                    dve.tensor_tensor(col(x_tok, j, D), col(x_tok, j, D), col(n_tok, j, D),
                                      ALU.add).then_inc(x_updated, 1)
                for j in range(TT):
                    dve.wait_ge(x_updated, TT * a + j + 1)
                    norm_stats("mid", a, j, col(x_tok, j, D))
                norm_moments("mid", a, range(TT))
                add_eps("mid", a)

            def norm_mid_apply(a):
                for j in range(TT):
                    norm_apply("mid", a, j, col(n_tok, j, D), col(x_tok, j, D))

            def finish(f):
                dve.wait_ge(out_stored, 16 * f + 16)
                dve.wait_ge(ff_psum, 2 * f + 2)
                for j in range(TT):
                    dve.tensor_tensor(col(y_tok, j, D), main[2 + j // 2][:, (j % 2) * D:(j % 2 + 1) * D],
                                      w3_scale[:, :], ALU.mult).then_inc(ff_read, 1)
                for j in range(TT):
                    dve.wait_ge(ff_read, TT * (f + 1) + j + 1)
                    norm_stats("out", f, j, col(y_tok, j, D))
                norm_moments("out", f, range(TT))
                add_eps("out", f)
                for j in range(TT):
                    norm_apply("out", f, j, col(y_tok, j, D), col(y_tok, j, D))
                for j in range(TT):
                    dve.wait_ge(normed["out"], TT * f + j + 1)
                    dve.tensor_tensor(col(y_tok, j, D), col(y_tok, j, D), col(resid, j, D),
                                      ALU.add).then_inc(out_set, 1)

            def keep_resid(f, a):
                if f is not None:
                    dve.wait_ge(out_set, TT * f + TT)
                dve.tensor_copy(resid[:, :], x_tok[:, :]).then_inc(resid_kept, 1)

            def body(f, a):
                if f is not None:
                    first_gated(f, 0)
                    for o in range(1, HT):
                        first_gated(f, o)
                        first_low(f, o - 1)
                        if a is not None and o == 2:
                            norm_x_stats(a)
                        if a is not None and o == 4:
                            norm_x_apply(a)
                    first_low(f, HT - 1)
                else:
                    norm_x_stats(a)
                    norm_x_apply(a)
                if a is not None:
                    for k in range(DT):
                        low(col(xT_lo, k), side[k][:, :], col(xT_hi, k), xT_hi_set,
                            DT * a + k + 1, xT_lo_set)
                if f is not None:
                    hidden(f, 1, 0)
                if a is not None:
                    for e in range(DT):
                        low(col(qT_lo, e), side[2 + e][:, :], col(qT_hi, e), q_hi_set,
                            DT * a + e + 1, q_lo_set, scale=SCORE_SCALE)
                if f is not None:
                    hidden(f, 1, 1)
                if a is not None:
                    for h in range(2):
                        low(col(v_lo, h), side[h][:, :], col(v_hi, h), v_hi_set,
                            2 * a + h + 1, v_lo_set)
                if f is not None:
                    hidden(f, 1, 2)
                if a is not None:
                    row_maxima(a, 0)
                    row_maxima(a, 1)
                if f is not None:
                    hidden(f, 1, 3)
                if a is not None:
                    row_maxima(a, 2)
                    row_maxima(a, 3)
                if f is not None:
                    hidden(f, 1, 4)
                if a is not None:
                    probs_low(a, 0)
                    probs_low(a, 1)
                if f is not None:
                    hidden(f, 1, 5)
                if a is not None:
                    probs_low(a, 2)
                if f is not None:
                    hidden(f, 1, 6)
                if a is not None:
                    probs_low(a, 3)
                if f is not None:
                    hidden(f, 1, 7)
                    hidden(f, 2, 0)
                if a is not None:
                    norm_att_stats(a, 0)
                    norm_att_stats(a, 1)
                    norm_att_root(a)
                if f is not None:
                    hidden(f, 2, 1)
                if a is not None:
                    update_x(a)
                if f is not None:
                    hidden(f, 2, 2)
                    hidden(f, 2, 3)
                if a is not None:
                    norm_mid_apply(a)
                if f is not None:
                    for o in range(4, HT):
                        hidden(f, 2, o)
                if a is not None:
                    for k in range(DT):
                        low(col(fT_lo, k), side[k][:, :], col(fT_hi, k), fT_hi_set,
                            DT * a + k + 1, fT_lo_set)
                if f is not None:
                    finish(f)
                if a is not None:
                    keep_resid(f, a)

            def set_flags():
                dve.wait_ge(piece_squared, len(pieces))
                dve.tensor_tensor(low_squares[:, :].rearrange("p (g n) -> p g n", n=P),
                                  main[1][:, :].rearrange("p (g n) -> p g n", n=P),
                                  ident[:, :].unsqueeze(1).to_broadcast([P, len(LAYERS), P]),
                                  ALU.mult).then_inc(low_squares_set, 1)
                dve.wait_ge(low_squares_set, 1)
                dve.tensor_reduce(low_sum[:, :], low_squares[:, :].rearrange("p (g n) -> p g n", n=P),
                                  AX.X, ALU.add).then_inc(low_sum_set, 1)
                dve.wait_ge(low_sum_psum, 1)
                dve.tensor_copy(low_flag[0:1, :], main[0][0:1, 0:len(LAYERS)]).then_inc(low_flag_set, 1)
                dve.wait_ge(piece_rounded, len(pieces))

            dve.wait_ge(const_set, 7)
            dve.wait_ge(dense_hi_set, 1)
            dve.tensor_tensor(dense_lo[:, :], dense_raw[:, :], dense_hi[:, :].bitcast(fp32),
                              ALU.subtract).then_inc(dense_lo_set, 1)
            body(None, 0)
            set_flags()
            with dve.Fori(0, CHUNKS - 1) as i:
                body(i, i + 1)
            body(CHUNKS - 1, None)

        @block.tensor
        def _(pe):
            def three_pass(dst, lhs, rhs, start, stop):
                pe.matmul(dst, lhs[0], rhs[0], start=start, stop=False)
                pe.matmul(dst, lhs[0], rhs[1], start=False, stop=False)
                return pe.matmul(dst, lhs[1], rhs[0], start=False, stop=stop)

            def square_pieces(first, last):
                for n in range(first, last):
                    g = [pieces[n][0] in names for names in LAYERS].index(True)
                    new = n == 0 or pieces[n - 1][0] not in LAYERS[g]
                    end = n == len(pieces) - 1 or pieces[n + 1][0] not in LAYERS[g]
                    pe.wait_ge(piece_loaded[n % SLOTS], 16 * (n // SLOTS + 1))
                    for c in range(PIECE // P):
                        half = low_halves(n, c)
                        last_mm = pe.matmul(main[1][:, g * P:(g + 1) * P], half, half,
                                            start=new and c == 0, stop=end and c == PIECE // P - 1)
                    last_mm.then_inc(piece_squared, 1)

            def act_by_float32(dst, activations, weights, lhs_is_weight, start, stop):
                activations = activations.bitcast(fp32)
                lhs, rhs = (weights, activations) if lhs_is_weight else (activations, weights)
                return pe.matmul(dst, lhs, rhs, start=start, stop=stop)

            def transposes(a, n, done):
                pe.wait_ge(normed[n], TT * a + TT)
                for k in range(DT):
                    for j in range(TT):
                        last = pe.transpose(side[k][:, j * P:(j + 1) * P],
                                            n_tok[:, j * D + k * P:j * D + (k + 1) * P], ident[:, :])
                    last.then_inc(done, 1)

            def pair(hi, lo, first, cols):
                return hi[:, first:first + cols], lo[:, first:first + cols]

            def queries(a):
                pe.wait_ge(xT_lo_set, DT * a + DT)
                for e in range(DT):
                    for k in range(DT):
                        last = three_pass(side[2 + e][:, :], pair(dense_hi, dense_lo, k * D + e * P, P),
                                          pair(xT_hi, xT_lo, k * S, S), k == 0, k == DT - 1)
                    last.then_inc(q_psum, 1)

            def values(a):
                for t in range(TT):
                    for k in range(DT):
                        last = three_pass(side[t // 2][:, (t % 2) * D:(t % 2 + 1) * D],
                                          pair(xT_hi, xT_lo, k * S + t * P, P),
                                          pair(dense_hi, dense_lo, (DT + k) * D, D),
                                          k == 0, k == DT - 1)
                    if t % 2:
                        last.then_inc(v_psum, 1)

            def scores(a, j):
                if j == 0:
                    pe.wait_ge(q_lo_set, DT * a + DT)
                if j >= 2:
                    pe.wait_ge(v_lo_set, 2 * a + j - 1)
                for k in range(DT):
                    last = three_pass(side[(j + 2) % 4][:, 0:(j + 1) * P],
                                      pair(qT_hi, qT_lo, k * S + j * P, P),
                                      pair(xT_hi, xT_lo, k * S, (j + 1) * P), k == 0, k == DT - 1)
                last.then_inc(scores_psum, 1)

            def probs_transposed(a, j):
                pe.wait_ge(probs_set, TT * a + j + 1)
                for t in range(j + 1):
                    last = pe.transpose(side[(j + 2) % 4][:, t * P:(t + 1) * P],
                                        probs[:, TRI[j] + t * P:TRI[j] + (t + 1) * P], ident[:, :])
                last.then_inc(pT_psum, 1)

            def attend(a, j):
                pe.wait_ge(pT_lo_set, TT * a + j + 1)
                for t in range(j + 1):
                    last = three_pass(side[2 + j // 2][:, (j % 2) * D:(j % 2 + 1) * D],
                                      pair(pT_hi, pT_lo, TRI[j] + t * P, P),
                                      pair(v_hi, v_lo, t * D, D), t == 0, t == j)
                if j % 2:
                    last.then_inc(att_psum, 1)

            def first_layer(f, o, full):
                if full:
                    pe.wait_ge(w_tile_loaded[0], 32 * (HT * f + o + 1))
                for part, name, done in ((0, "w1", gate_psum), (1, "w2", lin_psum)):
                    if o >= 2:
                        pe.wait_ge((gate_read, lin_read)[part], HT * f + o - 1)
                    for k in range(DT):
                        for src in (fT_hi, fT_lo):
                            dst, start, stop = (main[2 * (o % 2) + part][:, :],
                                                k == 0 and src is fT_hi, k == DT - 1 and src is fT_lo)
                            if full:
                                last = act_by_float32(dst, col(src, k), col(y_tok, part * DT + k, P),
                                                      True, start, stop)
                            else:
                                last = pe.matmul(dst, w_tile(name, k, o * P, P), col(src, k),
                                                 start=start, stop=stop)
                    last.then_inc(done, 1)

            def hidden(f, n, o, full):
                if o >= 4:
                    pe.wait_ge(gelu_set[n], HT * f + o - 3)
                elif n == 2:
                    pe.wait_ge(gelu_set[1], HT * f + o + 5)
                else:
                    pe.wait_ge((gate_read, lin_read)[o % 2], HT * f + HT - 1 + o // 2)
                if full:
                    pe.wait_ge(w_tile_loaded[n], 16 * (HT * f + o + 1))
                for k in range(HT):
                    for src, ready in ((hid_hi, hi_set), (hid_lo, lo_set)):
                        if o == 0:
                            pe.wait_ge(ready[n - 1], HT * f + k + 1)
                        start, stop = k == 0 and src is hid_hi, k == HT - 1 and src is hid_lo
                        x = col(src[(n - 1) % 2], k)
                        if full:
                            last = act_by_float32(main[o % 4][:, :], x, col(y_tok, k, P), True,
                                                  start, stop)
                        else:
                            last = pe.matmul(main[o % 4][:, :], w_tile(f"h{n}", k, o * P, P), x,
                                             start=start, stop=stop)
                last.then_inc(hid_psum[n], 1)

            def last_layer(f, j, full):
                if j % 2 == 0:
                    pe.wait_ge(gelu_set[2], HT * f + HT - 1 + j // 2)
                for k in range(HT):
                    if full and k % (HT // 2) == 0:
                        pe.wait_ge(w_tile_loaded[3], 16 * (HT * f + 2 * j + k // (HT // 2) + 1))
                    for src, ready in ((hid_hi, hi_set), (hid_lo, lo_set)):
                        if j == 0:
                            pe.wait_ge(ready[2], HT * f + k + 1)
                        dst = main[2 + j // 2][:, (j % 2) * D:(j % 2 + 1) * D]
                        start, stop = k == 0 and src is hid_hi, k == HT - 1 and src is hid_lo
                        x = src[0][:, k * S + j * P:k * S + (j + 1) * P]
                        if full:
                            last = act_by_float32(dst, x, col(y_tok, k % (HT // 2), D), False,
                                                  start, stop)
                        else:
                            last = pe.matmul(dst, x, w_tile("w3", k, 0, D), start=start, stop=stop)
                    if full and (k == HT // 2 - 1 or (k == HT - 1 and j % 2 == 0)):
                        last.then_inc(w3_half_used, 1)
                if j % 2:
                    last.then_inc(ff_psum, 1)

            def either(flag, pieces):
                with pe.If_eq(flag, 0):
                    pieces(False)
                with pe.Else():
                    pieces(True)

            flags = [pe.alloc_register(f"pe_low_{g}") for g in range(len(LAYERS))]

            def body(f, a):
                if f is not None:
                    pe.wait_ge(fT_lo_set, DT * f + DT)

                    def layer_0(full):
                        for o in range(HT):
                            if o == 1:
                                pe.wait_ge(ff_read, TT * f + TT)
                            first_layer(f, o, full)
                    either(flags[0], layer_0)
                if a is not None:
                    transposes(a, "x", xT_psum)

                def layer_1(full):
                    if f is not None:
                        hidden(f, 1, 0, full)
                    if a is not None:
                        queries(a)
                    if f is not None:
                        hidden(f, 1, 1, full)
                    if a is not None:
                        values(a)
                    if f is not None:
                        hidden(f, 1, 2, full)
                    if a is not None:
                        scores(a, 0)
                        scores(a, 1)
                    if f is not None:
                        hidden(f, 1, 3, full)
                    if a is not None:
                        scores(a, 2)
                        scores(a, 3)
                    if f is not None:
                        hidden(f, 1, 4, full)
                    if a is not None:
                        probs_transposed(a, 0)
                        probs_transposed(a, 1)
                    if f is not None:
                        hidden(f, 1, 5, full)
                    if a is not None:
                        probs_transposed(a, 2)
                        attend(a, 0)
                        attend(a, 1)
                    if f is not None:
                        hidden(f, 1, 6, full)
                    if a is not None:
                        probs_transposed(a, 3)
                    if f is not None:
                        hidden(f, 1, 7, full)

                def layer_2(full):
                    if f is not None:
                        hidden(f, 2, 0, full)
                    if a is not None:
                        attend(a, 2)
                        attend(a, 3)
                    if f is not None:
                        for o in range(1, HT):
                            hidden(f, 2, o, full)

                def layer_3(full):
                    for j in range(TT):
                        last_layer(f, j, full)

                if f is None:
                    layer_1(False)
                    layer_2(False)
                    transposes(a, "mid", fT_psum)
                    return
                either(flags[1], layer_1)
                either(flags[2], layer_2)
                if a is not None:
                    transposes(a, "mid", fT_psum)
                either(flags[3], layer_3)

            pe.wait_ge(const_set, 7)
            pe.wait_ge(dense_lo_set, 1)
            body(None, 0)
            square_pieces(0, len(pieces))
            pe.wait_ge(low_sum_set, 1)
            pe.matmul(main[0][0:1, 0:len(LAYERS)], ones[:, :], low_sum[:, :], start=True,
                      stop=True).then_inc(low_sum_psum, 1)
            pe.wait_ge(piece_rounded, len(pieces))
            pe.wait_ge(low_flag_set, 1)
            for g, reg in enumerate(flags):
                pe.reg_load(reg, low_flag[0:1, g:g + 1].bitcast(i32))
            with pe.Fori(0, CHUNKS - 1) as i:
                body(i, i + 1)
            body(CHUNKS - 1, None)


def kernel(L0_attn_input_data, L0_attn_qk, L0_attn_ov, L0_ffn_w1_w, L0_ffn_w1_s, L0_ffn_w2_w,
           L0_ffn_w2_s, L0_ffn_h1_w, L0_ffn_h1_s, L0_ffn_h2_w, L0_ffn_h2_s, L0_ffn_w3_w,
           L0_ffn_w3_s):
    import numpy as np
    import concourse.bacc as bacc
    from concourse.bass_utils import run_bass_kernel_spmd

    def rows(w):
        w = np.asarray(w)
        return np.ascontiguousarray(w.reshape(-1, P, w.shape[1]).transpose(1, 0, 2)).reshape(P, -1)

    def per_feature(s):
        return np.asarray(s).reshape(-1, P).T

    arrays = {
        "x": np.ascontiguousarray(L0_attn_input_data),
        "qk": rows(L0_attn_qk),
        "ov": rows(L0_attn_ov),
        "w1": rows(np.asarray(L0_ffn_w1_w).T),
        "w2": rows(np.asarray(L0_ffn_w2_w).T),
        "h1": rows(np.asarray(L0_ffn_h1_w).T),
        "h2": rows(np.asarray(L0_ffn_h2_w).T),
        "w3": rows(np.asarray(L0_ffn_w3_w).T),
        "scales": np.ascontiguousarray(np.concatenate(
            [per_feature(s) for s in (L0_ffn_w1_s, L0_ffn_w2_s, L0_ffn_h1_s, L0_ffn_h2_s)], axis=1)),
        "w3_scale": np.ascontiguousarray(L0_ffn_w3_s),
    }
    nc = bacc.Bacc("TRN2", target_bir_lowering=False, num_devices=1)
    args = [nc.dram_tensor(f"in_{n}", a.shape, mybir.dt.from_np(a.dtype), kind="ExternalInput").ap()
            for n, a in arrays.items()]
    shape = arrays["x"].shape
    out = nc.dram_tensor("out", shape, mybir.dt.float32, kind="ExternalOutput").ap()
    sandwich_kernel(nc, *args, out)
    r = run_bass_kernel_spmd(nc, [{f"in_{n}": a for n, a in arrays.items()}], core_ids=[0])
    return r.results[0]["out"]
```

```python
import concourse.bass as bass
from concourse import mybir
from contextlib import ExitStack

P = 128


def sandwich_kernel(nc, x_in, qk_in, ov_in, w1_in, w2_in, h1_in, h2_in, w3_in,
                    scales_in, w3_scale_in, out):
    fp32, fp32r = mybir.dt.float32, mybir.dt.float32r
    bf16, u16, i32 = mybir.dt.bfloat16, mybir.dt.uint16, mybir.dt.int32
    ALU, ACT, AX = mybir.AluOpType, mybir.ActivationFunctionType, mybir.AxisListType

    CHUNKS, S, D = x_in.shape
    HID = w1_in.shape[1] // (D // P)
    TT = S // P
    DT = D // P
    HT = HID // P
    EPS = 1e-5
    SCORE_SCALE = float(D) ** -0.5
    MASKED = -3.0e38
    BANK = 512

    TRI = [7 * P, 2 * P, 4 * P, 0]

    at = [(nc.sbuf_base + 63) // 64 * 64]

    def place(name, cols, dtype=fp32, over=None):
        offset = at[0] if over is None else over
        t = nc.alloc_sbuf_tensor_at(name, [P, cols], dtype, offset=offset)
        if over is None:
            at[0] += (cols * 4 + 31) // 32 * 32
            assert at[0] <= nc.sbuf_usable_end
        return t, offset

    W_PARTS = [("w1", w1_in), ("w2", w2_in), ("h1", h1_in), ("h2", h2_in), ("w3", w3_in)]
    W_COLS = sum(src.shape[1] for _, src in W_PARTS)
    w = place("w", W_COLS, fp32r)[0]
    w_first = {}
    for name, _ in W_PARTS:
        w_first[name] = sum(src.shape[1] for _, src in W_PARTS[:len(w_first)])
    PIECE = 2048
    SLOTS = 4 * HT * S // PIECE
    pieces = [(n, src, c) for n, src in W_PARTS for c in range(0, src.shape[1], PIECE)]
    LAYERS = [("w1", "w2"), ("h1",), ("h2",), ("w3",)]

    dense_hi = place("dense_hi", 2 * DT * D, fp32r)[0]
    dense_lo = place("dense_lo", 2 * DT * D, fp32r)[0]
    stage = place("stage", SLOTS * PIECE, over=at[0])[0]
    hid_hi = [place(f"hid{n}_hi", HT * S, fp32r)[0] for n in range(2)]
    hid_lo = [place(f"hid{n}_lo", HT * S, fp32r)[0] for n in range(2)]
    hid_new = place("hid_new", 2 * S)[0]
    x_tok = place("x_tok", TT * D)[0]
    resid = place("resid", TT * D)[0]
    y_tok, y_at = place("y_tok", TT * D)
    n_tok, n_at = place("n_tok", TT * D)
    probs = place("probs", TT * D, over=n_at)[0]
    xT_hi, xT_hi_at = place("xT_hi", DT * S, fp32r)
    xT_lo, xT_lo_at = place("xT_lo", DT * S, fp32r)
    pT_hi = place("pT_hi", DT * S, fp32r, over=xT_hi_at)[0]
    pT_lo = place("pT_lo", DT * S, fp32r, over=xT_lo_at)[0]
    qT_hi, qT_hi_at = place("qT_hi", DT * S, fp32r)
    qT_lo, qT_lo_at = place("qT_lo", DT * S, fp32r)
    fT_hi = place("fT_hi", DT * S, fp32r, over=qT_hi_at)[0]
    fT_lo = place("fT_lo", DT * S, fp32r, over=qT_lo_at)[0]
    v_hi = place("v_hi", TT * D, fp32r)[0]
    v_lo = place("v_lo", TT * D, fp32r)[0]
    dense_raw = place("dense_raw", 2 * DT * D, over=y_at)[0]

    ident = place("ident", P)[0]
    causal = place("causal", P)[0]
    w3_scale = place("w3_scale", D)[0]
    scales = place("scales", 4 * HT)[0]
    ones = place("ones", 1)[0]
    wait_here = place("wait_here", 2)[0]
    first_counts = place("first_counts", 2)[0]
    neg_half = place("neg_half", TT)[0]
    row_max = place("row_max", TT)[0]
    row_sum = place("row_sum", TT)[0]
    sum_eps = place("sum_eps", TT)[0]
    low_sum = place("low_sum", len(pieces))[0]
    low_flag = place("low_flag", len(LAYERS))[0]
    NORMS = ["x", "att", "mid", "out"]
    stats, moments, var_eps, rstd = {}, {}, {}, {}
    for n in NORMS:
        stats[n] = place(f"{n}_stats", TT * 6)[0]
        moments[n] = place(f"{n}_moments", TT * 2)[0]
        var_eps[n] = place(f"{n}_var_eps", TT)[0]
        rstd[n] = place(f"{n}_rstd", TT)[0]

    def w_tile(name, k, first, cols):
        c = w_first[name] + k * (D if name == "w3" else HID) + first
        return w[:, c:c + cols]

    def piece_slot(n):
        return stage[:, n % SLOTS * PIECE:(n % SLOTS + 1) * PIECE]

    def col(t, i, n=BANK):
        return t[:, i * n:(i + 1) * n]

    ctx = ExitStack()
    with ctx:
        main = [ctx.enter_context(nc.psum_tensor(f"main{i}", [P, BANK], fp32)) for i in range(4)]
        side = [ctx.enter_context(nc.psum_tensor(f"side{i}", [P, BANK], fp32)) for i in range(4)]

        def sem(name):
            return ctx.enter_context(nc.semaphore(name))

        x_loaded, out_stored = sem("x_loaded"), sem("out_stored")
        dense_loaded, scales_loaded = sem("dense_loaded"), sem("scales_loaded")
        piece_loaded = [sem(f"piece_loaded{i}") for i in range(SLOTS)]
        w_tile_loaded = [sem(f"w_tile{g}_loaded") for g in range(len(LAYERS))]
        const_set, dense_hi_set, dense_lo_set = sem("const_set"), sem("dense_hi_set"), sem("dense_lo_set")
        piece_rounded, piece_summed = sem("piece_rounded"), sem("piece_summed")
        low_sum_psum, low_flag_set = sem("low_sum_psum"), sem("low_flag_set")
        stats_set = {n: sem(f"{n}_stats_set") for n in NORMS}
        moments_set = {n: sem(f"{n}_moments_set") for n in NORMS}
        var_eps_set = {n: sem(f"{n}_var_eps_set") for n in NORMS}
        rstd_set = {n: sem(f"{n}_rstd_set") for n in NORMS}
        sum_eps_set = sem("sum_eps_set")
        normed = {n: sem(f"{n}_normed") for n in NORMS}
        xT_psum, xT_hi_set, xT_lo_set = sem("xT_psum"), sem("xT_hi_set"), sem("xT_lo_set")
        q_psum, q_hi_set, q_lo_set = sem("q_psum"), sem("q_hi_set"), sem("q_lo_set")
        v_psum, v_hi_set, v_lo_set = sem("v_psum"), sem("v_hi_set"), sem("v_lo_set")
        scores_psum, masked, max_set, probs_set = (
            sem("scores_psum"), sem("masked"), sem("max_set"), sem("probs_set"))
        pT_psum, pT_hi_set, pT_lo_set = sem("pT_psum"), sem("pT_hi_set"), sem("pT_lo_set")
        att_psum = sem("att_psum")
        x_updated, resid_kept = sem("x_updated"), sem("resid_kept")
        fT_psum, fT_hi_set, fT_lo_set = sem("fT_psum"), sem("fT_hi_set"), sem("fT_lo_set")
        gate_psum, lin_psum, gate_read, lin_read = (
            sem("gate_psum"), sem("lin_psum"), sem("gate_read"), sem("lin_read"))
        hid_psum = [None, sem("hid1_psum"), sem("hid2_psum")]
        gelu_set = [None, sem("gelu1_set"), sem("gelu2_set")]
        hi_set = [sem(f"hid{n}_hi_set") for n in range(3)]
        lo_set = [sem(f"hid{n}_lo_set") for n in range(3)]
        ff_psum, ff_read = sem("ff_psum"), sem("ff_read")
        w3_half_used = sem("w3_half_used")
        out_set = sem("out_set")

        block = ctx.enter_context(nc.Block())

        def run(eng, body):
            body(None, 0)
            with eng.Fori(0, CHUNKS - 1) as i:
                body(i, i + 1)
            body(CHUNKS - 1, None)

        @block.sync
        def _(sp):
            def load_x(a):
                if not isinstance(a, int):
                    sp.wait_ge(resid_kept, a)
                sp.dma_start(x_tok[:, :].rearrange("p (j d) -> p j d", j=TT),
                             x_in[a, :, :].rearrange("(j p) d -> p j d", p=P)).then_inc(x_loaded, 16)

            def store(f):
                sp.wait_ge(out_set, TT * f + TT)
                sp.dma_start(out[f, :, :].rearrange("(j p) d -> p j d", p=P),
                             y_tok[:, :].rearrange("p (j d) -> p j d", j=TT)).then_inc(out_stored, 16)

            load_x(0)
            sp.dma_start(dense_raw[:, 0:DT * D], qk_in).then_inc(dense_loaded, 16)
            sp.dma_start(dense_raw[:, DT * D:2 * DT * D], ov_in).then_inc(dense_loaded, 16)
            sp.dma_start(scales[:, :], scales_in).then_inc(scales_loaded, 16)
            sp.dma_start(w3_scale[:, :], w3_scale_in.partition_broadcast(P)).then_inc(scales_loaded, 16)
            for n, (_, src, c) in enumerate(pieces):
                if n >= SLOTS:
                    sp.wait_ge(piece_rounded, n - SLOTS + 1)
                    sp.wait_ge(piece_summed, n - SLOTS + 1)
                sp.dma_start(piece_slot(n), src[:, c:c + PIECE]).then_inc(piece_loaded[n % SLOTS], 16)

            flags = [sp.alloc_register(f"sp_low_{g}") for g in range(len(LAYERS))]
            sp.wait_ge(low_flag_set, 1)
            for g, reg in enumerate(flags):
                sp.reg_load(reg, low_flag[0:1, g:g + 1].bitcast(i32))

            def weight_tiles(g, f, wait_for_place, layout):
                with sp.If_ne(flags[g], 0):
                    wait_for_place()
                    for n in range(HT):
                        if n > 0:
                            if g < 3:
                                sp.wait_ge((lin_psum, hid_psum[1], hid_psum[2])[g], HT * f + n)
                            elif n % 4 == 0:
                                sp.wait_ge(ff_psum, 2 * f + n // 4)
                            else:
                                sp.wait_ge(w3_half_used, (2 * TT - 2) * f + n - n // 4)
                        for dst, src in layout(n):
                            sp.dma_start(dst, src).then_inc(w_tile_loaded[g], 16)

            def columns(src, n):
                k = src.shape[1] // HID
                return src.rearrange("p (k o) -> p k o", k=k)[:, :, n * P:(n + 1) * P]

            def weight_tiles_0(a, f):
                def layout(n):
                    return [(n_tok[:, i * DT * P:(i + 1) * DT * P].rearrange("p (k o) -> p k o", k=DT),
                             columns(src, n)) for i, src in enumerate((w1_in, w2_in))]

                def free():
                    if f is None:
                        sp.wait_ge(fT_psum, DT * a + DT)
                    else:
                        sp.wait_ge(ff_psum, 2 * f + 2)
                        sp.wait_ge(fT_psum, DT * a + DT)
                weight_tiles(0, a, free, layout)

            def weight_tiles_123(f, a):
                for g, src in ((1, h1_in), (2, h2_in)):
                    def layout(n):
                        return [(y_tok[:, :].rearrange("p (k o) -> p k o", k=HT), columns(src, n))]

                    def free():
                        sp.wait_ge(out_stored, 16 * f + 16)
                        if g == 2:
                            sp.wait_ge(hid_psum[1], HT * f + HT)
                    weight_tiles(g, f, free, layout)

                def layout(n):
                    half = HT // 2 * D
                    return [(n_tok[:, 0:half], w3_in[:, n % 2 * half:(n % 2 + 1) * half])]

                def free():
                    if a is not None:
                        sp.wait_ge(fT_psum, DT * a + DT)
                weight_tiles(3, f, free, layout)

            weight_tiles_0(0, None)
            with sp.Fori(0, CHUNKS - 1) as i:
                load_x(i + 1)
                weight_tiles_123(i, i + 1)
                weight_tiles_0(i + 1, i)
                store(i)
            weight_tiles_123(CHUNKS - 1, None)
            store(CHUNKS - 1)
            sp.wait_ge(out_stored, 16 * CHUNKS + 16)

        @block.gpsimd
        def _(pool):
            pool.memset(ident[:, :], 0.0).then_inc(const_set, 1)
            pool.memset(causal[:, :], 0.0).then_inc(const_set, 1)
            pool.memset(ones[:, :], 1.0).then_inc(const_set, 1)
            pool.memset(neg_half[:, :], -0.5).then_inc(const_set, 1)
            pool.memset(wait_here[:, :], 0.0).then_inc(const_set, 1)
            pool.memset(first_counts[:, 0:1], 0.0).then_inc(out_stored, 16)
            pool.memset(first_counts[:, 1:2], 0.0).then_inc(ff_read, TT)
            pool.wait_ge(const_set, 5)
            pool.affine_select(out=ident[:, :], in_=ident[:, :], compare_op=ALU.not_equal, fill=1.0,
                               base=0, pattern=[[-1, P]], channel_multiplier=1).then_inc(const_set, 1)
            pool.affine_select(out=causal[:, :], in_=causal[:, :], compare_op=ALU.is_ge, fill=MASKED,
                               base=0, pattern=[[-1, P]], channel_multiplier=1).then_inc(const_set, 1)

            def root(n, c):
                pool.wait_ge(var_eps_set[n], c + 1)
                pool.tensor_tensor(rstd[n][:, :], var_eps[n][:, :], neg_half[:, :],
                                   ALU.pow).then_inc(rstd_set[n], 1)

            def body(f, a):
                if a is not None:
                    root("x", a)
                    root("att", a)
                    root("mid", a)
                if f is not None:
                    root("out", f)
                    for j in range(TT):
                        pool.wait_ge(normed["out"], TT * f + j + 1)
                        pool.tensor_tensor(col(y_tok, j, D), col(y_tok, j, D), col(resid, j, D),
                                           ALU.add).then_inc(out_set, 1)

            run(pool, body)

        @block.scalar
        def _(act):
            def high(dst, src, ready, count, done, scale=1.0):
                act.wait_ge(ready, count)
                act.activation(dst, src, ACT.Copy, scale=scale).then_inc(done, 1)

            def first_layer(f, o):
                act.wait_ge(gate_psum, HT * f + o + 1)
                if o >= 2:
                    act.wait_ge(lo_set[0], HT * f + o - 1)
                act.activation(col(hid_new, o % 2), main[2 * (o % 2)][:, :], ACT.Silu,
                               scale=scales[:, o:o + 1]).then_inc(gate_read, 1)
                if o >= 1:
                    first_high(f, o - 1)

            def first_high(f, o):
                act.wait_ge(lin_read, HT * f + o + 1)
                act.activation(col(hid_hi[0], o), col(hid_new, o % 2), ACT.Copy).then_inc(hi_set[0], 1)

            def hidden(f, n, o):
                act.wait_ge(hid_psum[n], HT * f + o + 1)
                if o >= 2:
                    act.wait_ge(lo_set[n], HT * f + o - 1)
                else:
                    act.wait_ge(lo_set[n - 1], HT * f + HT - 1 + o)
                act.activation(col(hid_new, o % 2), main[o % 4][:, :], ACT.Gelu,
                               scale=scales[:, (n + 1) * HT + o:(n + 1) * HT + o + 1]
                               ).then_inc(gelu_set[n], 1)

            def softmax(a, j):
                act.wait_ge(max_set, TT * a + j + 1)
                if j == 3:
                    act.wait_ge(pT_psum, TT * a + 2)
                w = (j + 1) * P
                act.activation(probs[:, TRI[j]:TRI[j] + w], side[(j + 2) % 4][:, 0:w], ACT.Exp,
                               bias=row_max[:, j:j + 1], accum_out=row_sum[:, j:j + 1]
                               ).then_inc(probs_set, 1)

            def probs_high(a, j):
                if j == 3:
                    act.wait_ge(att_psum, 2 * a + 1)
                w = (j + 1) * P
                high(pT_hi[:, TRI[j]:TRI[j] + w], side[(j + 2) % 4][:, 0:w], pT_psum,
                     TT * a + j + 1, pT_hi_set)

            def sum_piece(n):
                act.wait_ge(piece_loaded[n % SLOTS], 16 * (n // SLOTS + 1))
                if n > 0:
                    act.wait_ge(piece_summed, n)
                act.activation(hid_new[:, :].bitcast(bf16),
                               piece_slot(n).bitcast(u16).rearrange("p (n two) -> p n two", two=2)[:, :, 0],
                               ACT.Copy, accum_out=low_sum[:, n:n + 1]).then_inc(piece_summed, 1)

            def body(f, a):
                n = 0

                def between(count):
                    nonlocal n
                    if f is None:
                        for _ in range(count):
                            sum_piece(n)
                            n += 1

                def h(layer, *tiles):
                    if f is not None:
                        for o in tiles:
                            hidden(f, layer, o)

                h(1, 0, 1, 2, 3)
                if a is None:
                    h(1, 4, 5, 6, 7)
                    h(2, *range(HT))
                    return
                for k in range(DT):
                    high(col(xT_hi, k), side[k][:, :], xT_psum, DT * a + k + 1, xT_hi_set)
                between(2)
                h(1, 4)
                for e in range(DT):
                    high(col(qT_hi, e), side[2 + e][:, :], q_psum, DT * a + e + 1, q_hi_set,
                         scale=SCORE_SCALE)
                between(2)
                h(1, 5)
                for i in range(2):
                    high(col(v_hi, i), side[i][:, :], v_psum, 2 * a + i + 1, v_hi_set)
                h(1, 6)
                softmax(a, 0)
                softmax(a, 1)
                h(1, 7)
                softmax(a, 2)
                h(2, 0)
                probs_high(a, 0)
                probs_high(a, 1)
                softmax(a, 3)
                h(2, 1)
                probs_high(a, 2)
                h(2, 2)
                probs_high(a, 3)
                between(5)
                h(2, *range(3, HT))
                for k in range(DT):
                    high(col(fT_hi, k), side[k][:, :], fT_psum, DT * a + k + 1, fT_hi_set)
                between(2)
                for o in range(HT):
                    first_layer(a, o)
                first_high(a, HT - 1)

            act.wait_ge(dense_loaded, 32)
            act.activation(dense_hi[:, :], dense_raw[:, :], ACT.Copy).then_inc(dense_hi_set, 1)
            act.wait_ge(scales_loaded, 32)
            run(act, body)

        @block.vector
        def _(dve):
            def low(dst, src, hi, ready, count, done, scale=None):
                dve.wait_ge(ready, count)
                if scale is None:
                    ins = dve.tensor_tensor(dst, src, hi.bitcast(fp32), ALU.subtract)
                else:
                    ins = dve.scalar_tensor_tensor(dst, src, scale, hi.bitcast(fp32),
                                                   ALU.mult, ALU.subtract)
                ins.then_inc(done, 1)

            def norm_stats(n, c, j, src):
                dve.bn_stats(stats[n][:, 6 * j:6 * j + 6], src).then_inc(stats_set[n], 1)

            def norm_moments(n, c, tiles):
                dve.wait_ge(stats_set[n], TT * c + max(tiles) + 1)
                dve.tensor_copy(wait_here[0:1, 1:2], wait_here[0:1, 0:1])
                for j in tiles:
                    dve.bn_aggr(moments[n][:, 2 * j:2 * j + 2],
                                stats[n][:, 6 * j:6 * j + 6]).then_inc(moments_set[n], 1)

            def variances(n):
                return moments[n][:, :].rearrange("p (j m) -> p j m", m=2)[:, :, 1]

            def add_eps(n, c):
                dve.wait_ge(moments_set[n], TT * c + TT)
                dve.tensor_scalar(var_eps[n][:, :], variances(n), EPS, None,
                                  ALU.add).then_inc(var_eps_set[n], 1)

            def norm_apply(n, c, j, dst, src):
                if j == 0:
                    dve.wait_ge(rstd_set[n], c + 1)
                dve.tensor_scalar(dst, src, moments[n][:, 2 * j:2 * j + 1], rstd[n][:, j:j + 1],
                                  ALU.subtract, ALU.mult).then_inc(normed[n], 1)

            def norm_x_stats(a):
                dve.wait_ge(x_loaded, 16 * a + 16)
                for j in range(TT):
                    norm_stats("x", a, j, col(x_tok, j, D))
                norm_moments("x", a, range(TT))
                add_eps("x", a)

            def norm_x_apply(a):
                for j in range(TT):
                    norm_apply("x", a, j, col(n_tok, j, D), col(x_tok, j, D))

            def first_gated(f, o):
                dve.wait_ge(lin_psum, HT * f + o + 1)
                dve.wait_ge(gate_read, HT * f + o + 1)
                dve.scalar_tensor_tensor(col(hid_new, o % 2), main[2 * (o % 2) + 1][:, :],
                                         scales[:, HT + o:HT + o + 1], col(hid_new, o % 2),
                                         ALU.mult, ALU.mult).then_inc(lin_read, 1)

            def first_low(f, o):
                low(col(hid_lo[0], o), col(hid_new, o % 2), col(hid_hi[0], o), hi_set[0],
                    HT * f + o + 1, lo_set[0])

            def hidden(f, n, o):
                dve.wait_ge(gelu_set[n], HT * f + o + 1)
                dve.tensor_copy(col(hid_hi[n % 2], o), col(hid_new, o % 2)).then_inc(hi_set[n], 1)
                low(col(hid_lo[n % 2], o), col(hid_new, o % 2), col(hid_hi[n % 2], o), hi_set[n],
                    HT * f + o + 1, lo_set[n])

            def row_maxima(a, j):
                bank = side[(j + 2) % 4]
                dve.wait_ge(scores_psum, TT * a + j + 1)
                diag = bank[:, j * P:(j + 1) * P]
                dve.tensor_tensor(diag, diag, causal[:, :], ALU.add).then_inc(masked, 1)
                dve.wait_ge(masked, TT * a + j + 1)
                dve.tensor_reduce(row_max[:, j:j + 1], bank[:, 0:(j + 1) * P], AX.X, ALU.max,
                                  negate=True).then_inc(max_set, 1)

            def probs_low(a, j):
                w = (j + 1) * P
                low(pT_lo[:, TRI[j]:TRI[j] + w], side[(j + 2) % 4][:, 0:w],
                    pT_hi[:, TRI[j]:TRI[j] + w], pT_hi_set, TT * a + j + 1, pT_lo_set)

            def att_tile(j):
                return side[2 + j // 2][:, (j % 2) * D:(j % 2 + 1) * D]

            def norm_att_stats(a, h):
                dve.wait_ge(att_psum, 2 * a + h + 1)
                for j in (2 * h, 2 * h + 1):
                    norm_stats("att", a, j, att_tile(j))
                norm_moments("att", a, (2 * h, 2 * h + 1))

            def norm_att_root(a):
                dve.wait_ge(probs_set, TT * a + TT)
                dve.scalar_tensor_tensor(sum_eps[:, :], row_sum[:, :], EPS, row_sum[:, :],
                                         ALU.mult, ALU.mult).then_inc(sum_eps_set, 1)
                dve.wait_ge(sum_eps_set, a + 1)
                dve.wait_ge(moments_set["att"], TT * a + TT)
                dve.tensor_tensor(var_eps["att"][:, :], variances("att"), sum_eps[:, :],
                                  ALU.add).then_inc(var_eps_set["att"], 1)

            def update_x(a):
                for j in range(TT):
                    norm_apply("att", a, j, col(n_tok, j, D), att_tile(j))
                for j in range(TT):
                    dve.wait_ge(normed["att"], TT * a + j + 1)
                    dve.tensor_tensor(col(x_tok, j, D), col(x_tok, j, D), col(n_tok, j, D),
                                      ALU.add).then_inc(x_updated, 1)
                for j in range(TT):
                    dve.wait_ge(x_updated, TT * a + j + 1)
                    norm_stats("mid", a, j, col(x_tok, j, D))
                norm_moments("mid", a, range(TT))
                add_eps("mid", a)

            def norm_mid_apply(a):
                for j in range(TT):
                    norm_apply("mid", a, j, col(n_tok, j, D), col(x_tok, j, D))

            def read_out(f, h):
                if h == 0:
                    dve.wait_ge(out_stored, 16 * f + 16)
                dve.wait_ge(ff_psum, 2 * f + h + 1)
                for j in (2 * h, 2 * h + 1):
                    dve.tensor_tensor(col(y_tok, j, D), main[2 + h][:, (j % 2) * D:(j % 2 + 1) * D],
                                      w3_scale[:, :], ALU.mult).then_inc(ff_read, 1)

            def norm_out_stats(f, h):
                dve.wait_ge(ff_read, TT * (f + 1) + 2 * h + 2)
                for j in (2 * h, 2 * h + 1):
                    norm_stats("out", f, j, col(y_tok, j, D))
                norm_moments("out", f, (2 * h, 2 * h + 1))

            def norm_out_apply(f):
                for j in range(TT):
                    norm_apply("out", f, j, col(y_tok, j, D), col(y_tok, j, D))

            def keep_resid(f, a):
                if f is not None:
                    dve.wait_ge(out_set, TT * f + TT)
                dve.tensor_copy(resid[:, :], x_tok[:, :]).then_inc(resid_kept, 1)

            def round_piece(n):
                dve.wait_ge(piece_loaded[n % SLOTS], 16 * (n // SLOTS + 1))
                name, _, c = pieces[n]
                dve.tensor_copy(w[:, w_first[name] + c:w_first[name] + c + PIECE],
                                piece_slot(n)).then_inc(piece_rounded, 1)

            def set_flags():
                dve.wait_ge(low_sum_psum, 1)
                dve.tensor_copy(low_flag[0:1, :], main[0][0:1, 0:len(LAYERS)]).then_inc(low_flag_set, 1)

            def body(f, a):
                n = 0

                def between(count):
                    nonlocal n
                    if f is None:
                        for _ in range(count):
                            round_piece(n)
                            n += 1

                def h(layer, *tiles):
                    if f is not None:
                        for o in tiles:
                            hidden(f, layer, o)

                h(1, 0, 1)
                if a is None:
                    h(1, *range(2, HT))
                    h(2, *range(HT))
                    read_out(f, 0)
                    norm_out_stats(f, 0)
                    read_out(f, 1)
                    norm_out_stats(f, 1)
                    add_eps("out", f)
                    norm_out_apply(f)
                    return
                norm_x_stats(a)
                h(1, 2)
                norm_x_apply(a)
                between(1)
                h(1, 3)
                for k in range(DT):
                    low(col(xT_lo, k), side[k][:, :], col(xT_hi, k), xT_hi_set,
                        DT * a + k + 1, xT_lo_set)
                between(2)
                h(1, 4)
                for e in range(DT):
                    low(col(qT_lo, e), side[2 + e][:, :], col(qT_hi, e), q_hi_set,
                        DT * a + e + 1, q_lo_set, scale=SCORE_SCALE)
                between(1)
                h(1, 5)
                for i in range(2):
                    low(col(v_lo, i), side[i][:, :], col(v_hi, i), v_hi_set, 2 * a + i + 1, v_lo_set)
                h(1, 6)
                row_maxima(a, 0)
                row_maxima(a, 1)
                h(1, 7)
                row_maxima(a, 2)
                row_maxima(a, 3)
                h(2, 0)
                probs_low(a, 0)
                probs_low(a, 1)
                h(2, 1)
                probs_low(a, 2)
                h(2, 2)
                probs_low(a, 3)
                between(1)
                h(2, 3)
                norm_att_stats(a, 0)
                norm_att_stats(a, 1)
                norm_att_root(a)
                between(1)
                h(2, 4)
                update_x(a)
                between(1)
                h(2, 5)
                norm_mid_apply(a)
                between(2)
                h(2, 6, 7)
                for k in range(DT):
                    low(col(fT_lo, k), side[k][:, :], col(fT_hi, k), fT_hi_set,
                        DT * a + k + 1, fT_lo_set)
                if f is None:
                    between(2)
                    set_flags()
                else:
                    read_out(f, 0)
                    read_out(f, 1)
                for o in range(HT):
                    first_gated(a, o)
                    if o > 0:
                        first_low(a, o - 1)
                    if f is not None:
                        if o == 1:
                            norm_out_stats(f, 0)
                        if o == 2:
                            norm_out_stats(f, 1)
                            add_eps("out", f)
                        if o == 4:
                            norm_out_apply(f)
                first_low(a, HT - 1)
                keep_resid(f, a)

            dve.wait_ge(const_set, 7)
            dve.wait_ge(dense_hi_set, 1)
            dve.tensor_tensor(dense_lo[:, :], dense_raw[:, :], dense_hi[:, :].bitcast(fp32),
                              ALU.subtract).then_inc(dense_lo_set, 1)
            run(dve, body)

        @block.tensor
        def _(pe):
            def three_pass(dst, lhs, rhs, start, stop):
                pe.matmul(dst, lhs[0], rhs[0], start=start, stop=False)
                pe.matmul(dst, lhs[0], rhs[1], start=False, stop=False)
                return pe.matmul(dst, lhs[1], rhs[0], start=False, stop=stop)

            def by_float32(dst, activations, weights, lhs_is_weight, start, stop):
                activations = activations.bitcast(fp32)
                lhs, rhs = (weights, activations) if lhs_is_weight else (activations, weights)
                return pe.matmul(dst, lhs, rhs, start=start, stop=stop)

            def transposes(a, n, done):
                pe.wait_ge(normed[n], TT * a + TT)
                for k in range(DT):
                    for j in range(TT):
                        last = pe.transpose(side[k][:, j * P:(j + 1) * P],
                                            n_tok[:, j * D + k * P:j * D + (k + 1) * P], ident[:, :])
                    last.then_inc(done, 1)

            def pair(hi, lo, first, cols):
                return hi[:, first:first + cols], lo[:, first:first + cols]

            def queries(a):
                pe.wait_ge(xT_lo_set, DT * a + DT)
                for e in range(DT):
                    for k in range(DT):
                        last = three_pass(side[2 + e][:, :], pair(dense_hi, dense_lo, k * D + e * P, P),
                                          pair(xT_hi, xT_lo, k * S, S), k == 0, k == DT - 1)
                    last.then_inc(q_psum, 1)

            def values(a):
                for t in range(TT):
                    for k in range(DT):
                        last = three_pass(side[t // 2][:, (t % 2) * D:(t % 2 + 1) * D],
                                          pair(xT_hi, xT_lo, k * S + t * P, P),
                                          pair(dense_hi, dense_lo, (DT + k) * D, D),
                                          k == 0, k == DT - 1)
                    if t % 2:
                        last.then_inc(v_psum, 1)

            def scores(a, j):
                if j == 0:
                    pe.wait_ge(q_lo_set, DT * a + DT)
                if j >= 2:
                    pe.wait_ge(v_lo_set, 2 * a + j - 1)
                for k in range(DT):
                    last = three_pass(side[(j + 2) % 4][:, 0:(j + 1) * P],
                                      pair(qT_hi, qT_lo, k * S + j * P, P),
                                      pair(xT_hi, xT_lo, k * S, (j + 1) * P), k == 0, k == DT - 1)
                last.then_inc(scores_psum, 1)

            def probs_transposed(a, j):
                pe.wait_ge(probs_set, TT * a + j + 1)
                for t in range(j + 1):
                    last = pe.transpose(side[(j + 2) % 4][:, t * P:(t + 1) * P],
                                        probs[:, TRI[j] + t * P:TRI[j] + (t + 1) * P], ident[:, :])
                last.then_inc(pT_psum, 1)

            def attend(a, j):
                pe.wait_ge(pT_lo_set, TT * a + j + 1)
                for t in range(j + 1):
                    last = three_pass(side[2 + j // 2][:, (j % 2) * D:(j % 2 + 1) * D],
                                      pair(pT_hi, pT_lo, TRI[j] + t * P, P),
                                      pair(v_hi, v_lo, t * D, D), t == 0, t == j)
                if j % 2:
                    last.then_inc(att_psum, 1)

            def first_layer(f, o, full):
                if full:
                    pe.wait_ge(w_tile_loaded[0], 32 * (HT * f + o + 1))
                for part, name, done in ((0, "w1", gate_psum), (1, "w2", lin_psum)):
                    if o >= 2:
                        pe.wait_ge((gate_read, lin_read)[part], HT * f + o - 1)
                    for k in range(DT):
                        for src in (fT_hi, fT_lo):
                            dst, start, stop = (main[2 * (o % 2) + part][:, :],
                                                k == 0 and src is fT_hi, k == DT - 1 and src is fT_lo)
                            if full:
                                last = by_float32(dst, col(src, k), col(n_tok, part * DT + k, P),
                                                      True, start, stop)
                            else:
                                last = pe.matmul(dst, w_tile(name, k, o * P, P), col(src, k),
                                                 start=start, stop=stop)
                    last.then_inc(done, 1)

            def hidden(f, n, o, full):
                if o >= 4:
                    pe.wait_ge(gelu_set[n], HT * f + o - 3)
                elif n == 2:
                    pe.wait_ge(gelu_set[1], HT * f + o + 5)
                else:
                    pe.wait_ge((gate_read, lin_read)[o % 2], HT * f + HT - 1 + o // 2)
                if full:
                    pe.wait_ge(w_tile_loaded[n], 16 * (HT * f + o + 1))
                for k in range(HT):
                    for src, ready in ((hid_hi, hi_set), (hid_lo, lo_set)):
                        if o == 0:
                            pe.wait_ge(ready[n - 1], HT * f + k + 1)
                        start, stop = k == 0 and src is hid_hi, k == HT - 1 and src is hid_lo
                        x = col(src[(n - 1) % 2], k)
                        if full:
                            last = by_float32(main[o % 4][:, :], x, col(y_tok, k, P), True,
                                                  start, stop)
                        else:
                            last = pe.matmul(main[o % 4][:, :], w_tile(f"h{n}", k, o * P, P), x,
                                             start=start, stop=stop)
                last.then_inc(hid_psum[n], 1)

            def last_layer(f, j, full):
                if j % 2 == 0:
                    pe.wait_ge(gelu_set[2], HT * f + HT - 1 + j // 2)
                for k in range(HT):
                    if full and k % (HT // 2) == 0:
                        pe.wait_ge(w_tile_loaded[3], 16 * (HT * f + 2 * j + k // (HT // 2) + 1))
                    for src, ready in ((hid_hi, hi_set), (hid_lo, lo_set)):
                        if j == 0:
                            pe.wait_ge(ready[2], HT * f + k + 1)
                        dst = main[2 + j // 2][:, (j % 2) * D:(j % 2 + 1) * D]
                        start, stop = k == 0 and src is hid_hi, k == HT - 1 and src is hid_lo
                        x = src[0][:, k * S + j * P:k * S + (j + 1) * P]
                        if full:
                            last = by_float32(dst, x, col(n_tok, k % (HT // 2), D), False,
                                                  start, stop)
                        else:
                            last = pe.matmul(dst, x, w_tile("w3", k, 0, D), start=start, stop=stop)
                    if full and (k == HT // 2 - 1 or (k == HT - 1 and j % 2 == 0)):
                        last.then_inc(w3_half_used, 1)
                if j % 2:
                    last.then_inc(ff_psum, 1)

            def either(flag, pieces):
                with pe.If_eq(flag, 0):
                    pieces(False)
                with pe.Else():
                    pieces(True)

            flags = [pe.alloc_register(f"pe_low_{g}") for g in range(len(LAYERS))]

            def read_flags():
                pe.wait_ge(piece_summed, len(pieces))
                for g, names in enumerate(LAYERS):
                    mine = [n for n, piece in enumerate(pieces) if piece[0] in names]
                    for n in mine:
                        last = pe.matmul(main[0][0:1, g:g + 1], ones[:, :], low_sum[:, n:n + 1],
                                         start=n == mine[0], stop=n == mine[-1])
                last.then_inc(low_sum_psum, 1)
                pe.wait_ge(piece_rounded, len(pieces))
                pe.wait_ge(low_flag_set, 1)
                for g, reg in enumerate(flags):
                    pe.reg_load(reg, low_flag[0:1, g:g + 1].bitcast(i32))

            def body(f, a):
                def layer_0(full):
                    for o in range(HT):
                        if o == 1:
                            pe.wait_ge(ff_read, TT * a + TT)
                        first_layer(a, o, full)

                def layer_1(full):
                    def h(*tiles):
                        if f is not None:
                            for o in tiles:
                                hidden(f, 1, o, full)

                    h(0, 1, 2, 3)
                    if a is None:
                        h(4, 5, 6, 7)
                        return
                    transposes(a, "x", xT_psum)
                    h(4)
                    queries(a)
                    h(5)
                    values(a)
                    h(6)
                    scores(a, 0)
                    scores(a, 1)
                    h(7)
                    scores(a, 2)
                    scores(a, 3)

                def layer_2(full):
                    def h(*tiles):
                        if f is not None:
                            for o in tiles:
                                hidden(f, 2, o, full)

                    h(0)
                    if a is None:
                        h(*range(1, HT))
                        return
                    probs_transposed(a, 0)
                    probs_transposed(a, 1)
                    h(1)
                    probs_transposed(a, 2)
                    attend(a, 0)
                    attend(a, 1)
                    h(2)
                    probs_transposed(a, 3)
                    h(3)
                    attend(a, 2)
                    attend(a, 3)
                    h(*range(4, HT))

                def layer_3(full):
                    for j in range(TT):
                        last_layer(f, j, full)

                if f is None:
                    layer_1(False)
                    layer_2(False)
                    transposes(a, "mid", fT_psum)
                    read_flags()
                else:
                    either(flags[1], layer_1)
                    either(flags[2], layer_2)
                    if a is not None:
                        transposes(a, "mid", fT_psum)
                    either(flags[3], layer_3)
                if a is not None:
                    pe.wait_ge(fT_lo_set, DT * a + DT)
                    either(flags[0], layer_0)

            pe.wait_ge(const_set, 7)
            pe.wait_ge(dense_lo_set, 1)
            run(pe, body)


def kernel(L0_attn_input_data, L0_attn_qk, L0_attn_ov, L0_ffn_w1_w, L0_ffn_w1_s, L0_ffn_w2_w,
           L0_ffn_w2_s, L0_ffn_h1_w, L0_ffn_h1_s, L0_ffn_h2_w, L0_ffn_h2_s, L0_ffn_w3_w,
           L0_ffn_w3_s):
    import numpy as np
    import concourse.bacc as bacc
    from concourse.bass_utils import run_bass_kernel_spmd

    def rows(w):
        w = np.asarray(w)
        return np.ascontiguousarray(w.reshape(-1, P, w.shape[1]).transpose(1, 0, 2)).reshape(P, -1)

    def per_feature(s):
        return np.asarray(s).reshape(-1, P).T

    arrays = {
        "x": np.ascontiguousarray(L0_attn_input_data),
        "qk": rows(L0_attn_qk),
        "ov": rows(L0_attn_ov),
        "w1": rows(np.asarray(L0_ffn_w1_w).T),
        "w2": rows(np.asarray(L0_ffn_w2_w).T),
        "h1": rows(np.asarray(L0_ffn_h1_w).T),
        "h2": rows(np.asarray(L0_ffn_h2_w).T),
        "w3": rows(np.asarray(L0_ffn_w3_w).T),
        "scales": np.ascontiguousarray(np.concatenate(
            [per_feature(s) for s in (L0_ffn_w1_s, L0_ffn_w2_s, L0_ffn_h1_s, L0_ffn_h2_s)], axis=1)),
        "w3_scale": np.ascontiguousarray(L0_ffn_w3_s),
    }
    nc = bacc.Bacc("TRN2", target_bir_lowering=False, num_devices=1)
    args = [nc.dram_tensor(f"in_{n}", a.shape, mybir.dt.from_np(a.dtype), kind="ExternalInput").ap()
            for n, a in arrays.items()]
    shape = arrays["x"].shape
    out = nc.dram_tensor("out", shape, mybir.dt.float32, kind="ExternalOutput").ap()
    sandwich_kernel(nc, *args, out)
    r = run_bass_kernel_spmd(nc, [{f"in_{n}": a for n, a in arrays.items()}], core_ids=[0])
    return r.results[0]["out"]
```

```python
import concourse.bass as bass
from concourse import mybir
from contextlib import ExitStack

P = 128


def sandwich_kernel(nc, x_in, qk_in, ov_in, w1_in, w2_in, h1_in, h2_in, w3_in,
                    scales_in, w3_scale_in, out):
    fp32, fp32r = mybir.dt.float32, mybir.dt.float32r
    bf16, u16, i32 = mybir.dt.bfloat16, mybir.dt.uint16, mybir.dt.int32
    ALU, ACT, AX = mybir.AluOpType, mybir.ActivationFunctionType, mybir.AxisListType

    CHUNKS, S, D = x_in.shape
    HID = w1_in.shape[1] // (D // P)
    TT = S // P
    DT = D // P
    HT = HID // P
    EPS = 1e-5
    SCORE_SCALE = float(D) ** -0.5
    MASKED = -3.0e38
    BANK = 512

    TRI = [7 * P, 2 * P, 4 * P, 0]

    at = [(nc.sbuf_base + 63) // 64 * 64]

    def place(name, cols, dtype=fp32, over=None):
        offset = at[0] if over is None else over
        t = nc.alloc_sbuf_tensor_at(name, [P, cols], dtype, offset=offset)
        if over is None:
            at[0] += (cols * 4 + 31) // 32 * 32
            assert at[0] <= nc.sbuf_usable_end
        return t, offset

    W_PARTS = [("w1", w1_in), ("w2", w2_in), ("h1", h1_in), ("h2", h2_in), ("w3", w3_in)]
    W_COLS = sum(src.shape[1] for _, src in W_PARTS)
    w = place("w", W_COLS, fp32r)[0]
    w_first = {}
    for name, _ in W_PARTS:
        w_first[name] = sum(src.shape[1] for _, src in W_PARTS[:len(w_first)])
    PIECE = 2048
    SLOTS = 4 * HT * S // PIECE
    pieces = [(n, src, c) for n, src in W_PARTS for c in range(0, src.shape[1], PIECE)]
    EARLY = SLOTS // 2
    assert len(pieces) <= SLOTS + EARLY
    POOL_PIECES = [1, 3, 8, 9]
    DVE_PIECES = [n for n in range(len(pieces)) if n not in POOL_PIECES]
    DVE_SUMS = [8]
    ACT_SUMS = [n for n in range(len(pieces)) if n not in DVE_SUMS]
    LAYERS = [("w1", "w2"), ("h1",), ("h2",), ("w3",)]

    dense_hi = place("dense_hi", 2 * DT * D, fp32r)[0]
    dense_lo = place("dense_lo", 2 * DT * D, fp32r)[0]
    stage = place("stage", SLOTS * PIECE, over=at[0])[0]
    hid_hi, hid_lo = [], []
    for n in range(2):
        hid_hi.append(place(f"hid{n}_hi", HT * S, fp32r)[0])
        hid_lo.append(place(f"hid{n}_lo", HT * S, fp32r)[0])
    hid_new = place("hid_new", 2 * S)[0]
    x_tok = place("x_tok", TT * D)[0]
    resid = place("resid", TT * D)[0]
    y_tok, y_at = place("y_tok", TT * D)
    n_tok, n_at = place("n_tok", TT * D)
    probs = place("probs", TT * D, over=n_at)[0]
    xT_hi, xT_hi_at = place("xT_hi", DT * S, fp32r)
    xT_lo, xT_lo_at = place("xT_lo", DT * S, fp32r)
    pT_hi = place("pT_hi", DT * S, fp32r, over=xT_hi_at)[0]
    pT_lo = place("pT_lo", DT * S, fp32r, over=xT_lo_at)[0]
    GATES = 2 * DT
    gated = place("gated", GATES * S, over=xT_hi_at)[0]
    qT_hi, qT_hi_at = place("qT_hi", DT * S, fp32r)
    qT_lo, qT_lo_at = place("qT_lo", DT * S, fp32r)
    fT_hi = place("fT_hi", DT * S, fp32r, over=qT_hi_at)[0]
    fT_lo = place("fT_lo", DT * S, fp32r, over=qT_lo_at)[0]
    v_hi = place("v_hi", TT * D, fp32r)[0]
    v_lo = place("v_lo", TT * D, fp32r)[0]
    dense_raw = place("dense_raw", 2 * DT * D, over=y_at)[0]

    ident = place("ident", P)[0]
    causal = place("causal", P)[0]
    w3_scale = place("w3_scale", D)[0]
    scales = place("scales", 4 * HT)[0]
    ones = place("ones", 1)[0]
    wait_here = place("wait_here", 2)[0]
    first_counts = place("first_counts", 2)[0]
    neg_half = place("neg_half", TT)[0]
    row_max = place("row_max", TT)[0]
    row_sum = place("row_sum", TT)[0]
    sum_eps = place("sum_eps", TT)[0]
    low_sum = place("low_sum", len(pieces))[0]
    low_flag = place("low_flag", len(LAYERS))[0]
    NORMS = ["x", "att", "mid", "out"]
    stats, moments, var_eps, rstd = {}, {}, {}, {}
    for n in NORMS:
        stats[n] = place(f"{n}_stats", TT * 6)[0]
        moments[n] = place(f"{n}_moments", TT * 2)[0]
        var_eps[n] = place(f"{n}_var_eps", TT)[0]
        rstd[n] = place(f"{n}_rstd", TT)[0]

    def w_tile(name, k, first, cols):
        c = w_first[name] + k * (D if name == "w3" else HID) + first
        return w[:, c:c + cols]

    def slot_of(n):
        return n if n < SLOTS else n - SLOTS + EARLY

    def piece_slot(n):
        return stage[:, slot_of(n) * PIECE:(slot_of(n) + 1) * PIECE]

    def low_halves(n):
        return piece_slot(n).bitcast(u16).rearrange("p (n two) -> p n two", two=2)[:, :, 0]

    def count_before(some, n):
        return sum(m < n for m in some)

    def col(t, i, n=BANK):
        return t[:, i * n:(i + 1) * n]

    ctx = ExitStack()
    with ctx:
        main = [ctx.enter_context(nc.psum_tensor(f"main{i}", [P, BANK], fp32)) for i in range(4)]
        side = [ctx.enter_context(nc.psum_tensor(f"side{i}", [P, BANK], fp32)) for i in range(4)]

        out_bank = [side[2], side[3], main[2], main[3]]

        def sem(name):
            return ctx.enter_context(nc.semaphore(name))

        x_loaded, out_stored = sem("x_loaded"), sem("out_stored")
        dense_loaded, scales_loaded = sem("dense_loaded"), sem("scales_loaded")
        piece_loaded = [sem(f"piece_loaded{i}") for i in range(SLOTS)]
        w_tile_loaded = [sem(f"w_tile{g}_loaded") for g in range(len(LAYERS))]
        const_set, dense_hi_set, dense_lo_set = sem("const_set"), sem("dense_hi_set"), sem("dense_lo_set")
        pool_rounded, dve_rounded = sem("pool_rounded"), sem("dve_rounded")
        act_summed, dve_summed = sem("act_summed"), sem("dve_summed")
        low_sum_psum, low_flag_set = sem("low_sum_psum"), sem("low_flag_set")
        stats_set = {n: sem(f"{n}_stats_set") for n in NORMS}
        moments_set = {n: sem(f"{n}_moments_set") for n in NORMS}
        var_eps_set = {n: sem(f"{n}_var_eps_set") for n in NORMS}
        rstd_set = {n: sem(f"{n}_rstd_set") for n in NORMS}
        sum_eps_set = sem("sum_eps_set")
        normed = {n: sem(f"{n}_normed") for n in NORMS}
        xT_psum, xT_hi_set, xT_lo_set = sem("xT_psum"), sem("xT_hi_set"), sem("xT_lo_set")
        q_psum, q_hi_set, q_lo_set = sem("q_psum"), sem("q_hi_set"), sem("q_lo_set")
        v_psum, v_hi_set, v_lo_set = sem("v_psum"), sem("v_hi_set"), sem("v_lo_set")
        scores_psum, masked, max_set, probs_set = (
            sem("scores_psum"), sem("masked"), sem("max_set"), sem("probs_set"))
        pT_psum, pT_hi_set, pT_lo_set = sem("pT_psum"), sem("pT_hi_set"), sem("pT_lo_set")
        att_psum = sem("att_psum")
        x_updated, resid_kept = sem("x_updated"), sem("resid_kept")
        fT_psum, fT_hi_set, fT_lo_set = sem("fT_psum"), sem("fT_hi_set"), sem("fT_lo_set")
        gate_psum, lin_psum, gate_read, lin_read = (
            sem("gate_psum"), sem("lin_psum"), sem("gate_read"), sem("lin_read"))
        hid_psum = [None, sem("hid1_psum"), sem("hid2_psum")]
        gelu_set = [None, sem("gelu1_set"), sem("gelu2_set")]
        hi_set = [sem(f"hid{n}_hi_set") for n in range(3)]
        lo_set = [sem(f"hid{n}_lo_set") for n in range(3)]
        ff_psum, ff_read = sem("ff_psum"), sem("ff_read")
        w3_half_used = sem("w3_half_used")
        out_set = sem("out_set")

        block = ctx.enter_context(nc.Block())

        def run(eng, body):
            body(None, 0)
            with eng.Fori(0, CHUNKS - 1) as i:
                body(i, i + 1)
            body(CHUNKS - 1, None)

        FLAG_STAGES = [range(0, 1), range(1, len(LAYERS))]
        flag_psum = [main[0], side[2]]
        LAST_SUMS = HT - 3

        def read_flags(eng, flags, stage):
            eng.wait_ge(low_flag_set, stage + 1)
            for g in FLAG_STAGES[stage]:
                eng.reg_load(flags[g], low_flag[0:1, g:g + 1].bitcast(i32))

        def wait_piece(eng, n):
            eng.wait_ge(piece_loaded[slot_of(n)], 16 * (n // SLOTS + 1))

        def wait_rounded(eng, n):
            if count_before(POOL_PIECES, n) > 0:
                eng.wait_ge(pool_rounded, count_before(POOL_PIECES, n))
            eng.wait_ge(dve_rounded, count_before(DVE_PIECES, n))

        def wait_summed(eng, n):
            eng.wait_ge(act_summed, count_before(ACT_SUMS, n))
            if count_before(DVE_SUMS, n) > 0:
                eng.wait_ge(dve_summed, count_before(DVE_SUMS, n))

        def round_piece(eng, n, done):
            wait_piece(eng, n)
            name, _, c = pieces[n]
            eng.tensor_copy(w[:, w_first[name] + c:w_first[name] + c + PIECE],
                            piece_slot(n)).then_inc(done, 1)

        @block.sync
        def _(sp):
            def load_x(a):
                if not isinstance(a, int):
                    sp.wait_ge(resid_kept, a)
                sp.dma_start(x_tok[:, :].rearrange("p (j d) -> p j d", j=TT),
                             x_in[a, :, :].rearrange("(j p) d -> p j d", p=P)).then_inc(x_loaded, 16)

            def store(f, parts=1):
                n = TT // parts
                for h in range(parts):
                    sp.wait_ge(out_set, TT * f + (h + 1) * n)
                    sp.dma_start(out[f, h * n * P:(h + 1) * n * P, :].rearrange("(j p) d -> p j d", p=P),
                                 y_tok[:, h * n * D:(h + 1) * n * D].rearrange("p (j d) -> p j d", j=n)
                                 ).then_inc(out_stored, 16)

            load_x(0)
            sp.dma_start(dense_raw[:, 0:DT * D], qk_in).then_inc(dense_loaded, 16)
            sp.dma_start(dense_raw[:, DT * D:2 * DT * D], ov_in).then_inc(dense_loaded, 16)
            sp.dma_start(scales[:, :], scales_in).then_inc(scales_loaded, 16)
            sp.dma_start(w3_scale[:, :], w3_scale_in.partition_broadcast(P)).then_inc(scales_loaded, 16)
            for n, (_, src, c) in enumerate(pieces):
                if n >= SLOTS:
                    wait_rounded(sp, slot_of(n) + 1)
                    wait_summed(sp, slot_of(n) + 1)
                sp.dma_start(piece_slot(n), src[:, c:c + PIECE]).then_inc(piece_loaded[slot_of(n)], 16)

            flags = [sp.alloc_register(f"sp_low_{g}") for g in range(len(LAYERS))]

            def weight_tiles(g, f, wait_for_place, layout):
                with sp.If_ne(flags[g], 0):
                    wait_for_place()
                    for n in range(HT):
                        if n > 0:
                            if g < 3:
                                sp.wait_ge((lin_psum, hid_psum[1], hid_psum[2])[g], HT * f + n)
                            elif n % 2 == 0:
                                sp.wait_ge(ff_psum, TT * f + n // 2)
                            else:
                                sp.wait_ge(w3_half_used, TT * f + n // 2 + 1)
                        for dst, src in layout(n):
                            sp.dma_start(dst, src).then_inc(w_tile_loaded[g], 16)

            def columns(src, n):
                k = src.shape[1] // HID
                return src.rearrange("p (k o) -> p k o", k=k)[:, :, n * P:(n + 1) * P]

            def weight_tiles_0(a, f):
                def layout(n):
                    return [(n_tok[:, i * DT * P:(i + 1) * DT * P].rearrange("p (k o) -> p k o", k=DT),
                             columns(src, n)) for i, src in enumerate((w1_in, w2_in))]

                def free():
                    if f is None:
                        sp.wait_ge(fT_psum, DT * a + DT)
                    else:
                        sp.wait_ge(ff_psum, TT * f + TT)
                        sp.wait_ge(fT_psum, DT * a + DT)
                weight_tiles(0, a, free, layout)

            def weight_tiles_123(f, a):
                for g, src in ((1, h1_in), (2, h2_in)):
                    def layout(n):
                        return [(y_tok[:, :].rearrange("p (k o) -> p k o", k=HT), columns(src, n))]

                    def free():
                        sp.wait_ge(out_stored, 16 * f + 16)
                        if g == 2:
                            sp.wait_ge(hid_psum[1], HT * f + HT)
                    weight_tiles(g, f, free, layout)

                def layout(n):
                    half = HT // 2 * D
                    return [(n_tok[:, 0:half], w3_in[:, n % 2 * half:(n % 2 + 1) * half])]

                def free():
                    if a is not None:
                        sp.wait_ge(fT_psum, DT * a + DT)
                weight_tiles(3, f, free, layout)

            read_flags(sp, flags, 0)
            weight_tiles_0(0, None)
            read_flags(sp, flags, 1)
            with sp.Fori(0, CHUNKS - 1) as i:
                load_x(i + 1)
                weight_tiles_123(i, i + 1)
                weight_tiles_0(i + 1, i)
                store(i)
            weight_tiles_123(CHUNKS - 1, None)
            store(CHUNKS - 1, parts=2)
            sp.wait_ge(out_stored, 16 * CHUNKS + 32)

        @block.gpsimd
        def _(pool):
            pool.memset(ident[:, :], 0.0).then_inc(const_set, 1)
            pool.memset(causal[:, :], 0.0).then_inc(const_set, 1)
            pool.memset(ones[:, :], 1.0).then_inc(const_set, 1)
            pool.memset(neg_half[:, :], -0.5).then_inc(const_set, 1)
            pool.memset(wait_here[:, :], 0.0).then_inc(const_set, 1)
            pool.memset(first_counts[:, 0:1], 0.0).then_inc(out_stored, 16)
            pool.memset(first_counts[:, 1:2], 0.0).then_inc(ff_read, TT)
            pool.wait_ge(const_set, 5)
            pool.affine_select(out=ident[:, :], in_=ident[:, :], compare_op=ALU.not_equal, fill=1.0,
                               base=0, pattern=[[-1, P]], channel_multiplier=1).then_inc(const_set, 1)
            pool.affine_select(out=causal[:, :], in_=causal[:, :], compare_op=ALU.is_ge, fill=MASKED,
                               base=0, pattern=[[-1, P]], channel_multiplier=1).then_inc(const_set, 1)

            def roots(n, c):
                for h in range(2):
                    pool.wait_ge(var_eps_set[n], 2 * c + h + 1)
                    half = slice(2 * h, 2 * h + 2)
                    pool.tensor_tensor(rstd[n][:, half], var_eps[n][:, half], neg_half[:, half],
                                       ALU.pow).then_inc(rstd_set[n], 1)

            def body(f, a):
                if a is not None:
                    roots("x", a)
                    if f is None:
                        for n in POOL_PIECES[:2]:
                            round_piece(pool, n, pool_rounded)
                    roots("att", a)
                    roots("mid", a)
                    if f is None:
                        for n in POOL_PIECES[2:]:
                            round_piece(pool, n, pool_rounded)
                if f is not None:
                    roots("out", f)
                if f is not None and a is not None:
                    for j in range(TT):
                        pool.wait_ge(normed["out"], TT * f + j + 1)
                        pool.tensor_tensor(col(y_tok, j, D), col(y_tok, j, D), col(resid, j, D),
                                           ALU.add).then_inc(out_set, 1)

            run(pool, body)

        @block.scalar
        def _(act):
            def high(dst, src, ready, count, done, scale=1.0):
                act.wait_ge(ready, count)
                act.activation(dst, src, ACT.Copy, scale=scale).then_inc(done, 1)

            def first_layer(f, o):
                act.wait_ge(gate_psum, HT * f + o + 1)
                if o >= GATES:
                    act.wait_ge(lo_set[0], HT * f + o - GATES + 1)
                act.activation(col(gated, o % GATES), main[2 * (o % 2)][:, :], ACT.Silu,
                               scale=scales[:, o:o + 1]).then_inc(gate_read, 1)
                if o >= 1:
                    first_high(f, o - 1)

            def first_high(f, o):
                act.wait_ge(lin_read, HT * f + o + 1)
                act.activation(col(hid_hi[0], o), col(gated, o % GATES), ACT.Copy).then_inc(hi_set[0], 1)

            def hidden(f, n, o):
                act.wait_ge(hid_psum[n], HT * f + o + 1)
                if o >= 2:
                    act.wait_ge(lo_set[n], HT * f + o - 1)
                elif n == 2:
                    act.wait_ge(lo_set[1], HT * f + HT - 1 + o)
                act.activation(col(hid_new, o % 2), main[o % 4][:, :], ACT.Gelu,
                               scale=scales[:, (n + 1) * HT + o:(n + 1) * HT + o + 1]
                               ).then_inc(gelu_set[n], 1)

            def softmax(a, j):
                act.wait_ge(max_set, TT * a + j + 1)
                if j == 3:
                    act.wait_ge(pT_psum, TT * a + 2)
                w = (j + 1) * P
                act.activation(probs[:, TRI[j]:TRI[j] + w], side[(j + 2) % 4][:, 0:w], ACT.Exp,
                               bias=row_max[:, j:j + 1], accum_out=row_sum[:, j:j + 1]
                               ).then_inc(probs_set, 1)

            def probs_high(a, j):
                if j == 3:
                    act.wait_ge(att_psum, 2 * a + 1)
                w = (j + 1) * P
                high(pT_hi[:, TRI[j]:TRI[j] + w], side[(j + 2) % 4][:, 0:w], pT_psum,
                     TT * a + j + 1, pT_hi_set)

            def sum_piece(n):
                wait_piece(act, n)
                if n > 0:
                    act.wait_ge(act_summed, count_before(ACT_SUMS, n))
                act.activation(hid_new[:, :].bitcast(bf16), low_halves(n), ACT.Copy,
                               accum_out=low_sum[:, n:n + 1]).then_inc(act_summed, 1)

            def set_flags(stage):
                act.wait_ge(low_sum_psum, stage + 1)
                some = slice(FLAG_STAGES[stage].start, FLAG_STAGES[stage].stop)
                act.activation(low_flag[0:1, some], flag_psum[stage][0:1, some], ACT.Copy
                               ).then_inc(low_flag_set, 1)

            def body(f, a):
                n = 0

                def between(count):
                    nonlocal n
                    if f is None:
                        for _ in range(count):
                            sum_piece(ACT_SUMS[n])
                            n += 1

                def h(layer, *tiles):
                    if f is not None:
                        for o in tiles:
                            hidden(f, layer, o)

                h(1, 0, 1, 2, 3)
                if a is None:
                    h(1, 4, 5, 6, 7)
                    h(2, *range(HT))
                    return
                for k in range(DT):
                    high(col(xT_hi, k), side[k][:, :], xT_psum, DT * a + k + 1, xT_hi_set)
                between(2)
                h(1, 4)
                for e in range(DT):
                    high(col(qT_hi, e), side[2 + e][:, :], q_psum, DT * a + e + 1, q_hi_set,
                         scale=SCORE_SCALE)
                h(1, 5)
                for i in range(2):
                    high(col(v_hi, i), side[i][:, :], v_psum, 2 * a + i + 1, v_hi_set)
                between(1)
                h(1, 6)
                softmax(a, 0)
                softmax(a, 1)
                h(1, 7)
                softmax(a, 2)
                h(2, 0)
                probs_high(a, 0)
                probs_high(a, 1)
                softmax(a, 3)
                h(2, 1)
                probs_high(a, 2)
                h(2, 2)
                probs_high(a, 3)
                if f is None:
                    set_flags(0)
                between(4)
                h(2, *range(3, HT))
                for k in range(DT):
                    high(col(fT_hi, k), side[k][:, :], fT_psum, DT * a + k + 1, fT_hi_set)
                between(1)
                for o in range(HT):
                    first_layer(a, o)
                    if o in (1, 3):
                        between(1)
                    if f is None and o == LAST_SUMS + 1:
                        set_flags(1)
                first_high(a, HT - 1)

            act.wait_ge(dense_loaded, 32)
            act.activation(dense_hi[:, :], dense_raw[:, :], ACT.Copy).then_inc(dense_hi_set, 1)
            act.wait_ge(scales_loaded, 32)
            run(act, body)

        @block.vector
        def _(dve):
            def low(dst, src, hi, ready, count, done, scale=None):
                dve.wait_ge(ready, count)
                if scale is None:
                    ins = dve.tensor_tensor(dst, src, hi.bitcast(fp32), ALU.subtract)
                else:
                    ins = dve.scalar_tensor_tensor(dst, src, scale, hi.bitcast(fp32),
                                                   ALU.mult, ALU.subtract)
                ins.then_inc(done, 1)

            def norm_stats(n, c, h, src):
                for j in (2 * h, 2 * h + 1):
                    dve.bn_stats(stats[n][:, 6 * j:6 * j + 6], src(j)).then_inc(stats_set[n], 1)
                dve.wait_ge(stats_set[n], TT * c + 2 * h + 2)
                dve.tensor_copy(wait_here[0:1, 1:2], wait_here[0:1, 0:1])
                for j in (2 * h, 2 * h + 1):
                    dve.bn_aggr(moments[n][:, 2 * j:2 * j + 2],
                                stats[n][:, 6 * j:6 * j + 6]).then_inc(moments_set[n], 1)

            def variances(n, h):
                return moments[n][:, 4 * h:4 * h + 4].rearrange("p (j m) -> p j m", m=2)[:, :, 1]

            def add_eps(n, c, h):
                dve.wait_ge(moments_set[n], TT * c + 2 * h + 2)
                dve.tensor_scalar(var_eps[n][:, 2 * h:2 * h + 2], variances(n, h), EPS, None,
                                  ALU.add).then_inc(var_eps_set[n], 1)

            def norm_apply(n, c, h, dst, src):
                dve.wait_ge(rstd_set[n], 2 * c + h + 1)
                for j in (2 * h, 2 * h + 1):
                    dve.tensor_scalar(dst(j), src(j), moments[n][:, 2 * j:2 * j + 1],
                                      rstd[n][:, j:j + 1], ALU.subtract, ALU.mult
                                      ).then_inc(normed[n], 1)

            def x_tile(j):
                return col(x_tok, j, D)

            def n_tile(j):
                return col(n_tok, j, D)

            def y_tile(j):
                return col(y_tok, j, D)

            def norm_x_stats(a):
                dve.wait_ge(x_loaded, 16 * a + 16)
                for h in range(2):
                    norm_stats("x", a, h, x_tile)
                    add_eps("x", a, h)

            def norm_x_apply(a):
                for h in range(2):
                    norm_apply("x", a, h, n_tile, x_tile)

            def first_gated(f, o):
                dve.wait_ge(lin_psum, HT * f + o + 1)
                dve.wait_ge(gate_read, HT * f + o + 1)
                slot = col(gated, o % GATES)
                dve.scalar_tensor_tensor(slot, main[2 * (o % 2) + 1][:, :],
                                         scales[:, HT + o:HT + o + 1], slot,
                                         ALU.mult, ALU.mult).then_inc(lin_read, 1)

            def first_low(f, o):
                low(col(hid_lo[0], o), col(gated, o % GATES), col(hid_hi[0], o), hi_set[0],
                    HT * f + o + 1, lo_set[0])

            def hidden(f, n, o):
                dve.wait_ge(gelu_set[n], HT * f + o + 1)
                dve.tensor_copy(col(hid_hi[n % 2], o), col(hid_new, o % 2)).then_inc(hi_set[n], 1)
                low(col(hid_lo[n % 2], o), col(hid_new, o % 2), col(hid_hi[n % 2], o), hi_set[n],
                    HT * f + o + 1, lo_set[n])

            def row_maxima(a, j):
                bank = side[(j + 2) % 4]
                dve.wait_ge(scores_psum, TT * a + j + 1)
                diag = bank[:, j * P:(j + 1) * P]
                dve.tensor_tensor(diag, diag, causal[:, :], ALU.add).then_inc(masked, 1)
                dve.wait_ge(masked, TT * a + j + 1)
                dve.tensor_reduce(row_max[:, j:j + 1], bank[:, 0:(j + 1) * P], AX.X, ALU.max,
                                  negate=True).then_inc(max_set, 1)

            def probs_low(a, j):
                w = (j + 1) * P
                low(pT_lo[:, TRI[j]:TRI[j] + w], side[(j + 2) % 4][:, 0:w],
                    pT_hi[:, TRI[j]:TRI[j] + w], pT_hi_set, TT * a + j + 1, pT_lo_set)

            def att_tile(j):
                return side[2 + j // 2][:, (j % 2) * D:(j % 2 + 1) * D]

            def norm_att_stats(a, h):
                half = slice(2 * h, 2 * h + 2)
                dve.wait_ge(att_psum, 2 * a + h + 1)
                dve.scalar_tensor_tensor(sum_eps[:, half], row_sum[:, half], EPS, row_sum[:, half],
                                         ALU.mult, ALU.mult).then_inc(sum_eps_set, 1)
                norm_stats("att", a, h, att_tile)
                dve.wait_ge(sum_eps_set, 2 * a + h + 1)
                dve.wait_ge(moments_set["att"], TT * a + 2 * h + 2)
                dve.tensor_tensor(var_eps["att"][:, half], variances("att", h), sum_eps[:, half],
                                  ALU.add).then_inc(var_eps_set["att"], 1)

            def update_x(a, h):
                norm_apply("att", a, h, n_tile, att_tile)
                for j in (2 * h, 2 * h + 1):
                    dve.wait_ge(normed["att"], TT * a + j + 1)
                    dve.tensor_tensor(x_tile(j), x_tile(j), n_tile(j), ALU.add).then_inc(x_updated, 1)
                dve.wait_ge(x_updated, TT * a + 2 * h + 2)
                norm_stats("mid", a, h, x_tile)
                add_eps("mid", a, h)

            def norm_mid_apply(a, h):
                norm_apply("mid", a, h, n_tile, x_tile)

            def read_out(f, *tiles):
                for j in tiles:
                    if j == 0:
                        dve.wait_ge(out_stored, 16 * f + 16)
                    dve.wait_ge(ff_psum, TT * f + j + 1)
                    dve.tensor_tensor(y_tile(j), out_bank[j][:, 0:D], w3_scale[:, :],
                                      ALU.mult).then_inc(ff_read, 1)

            def norm_out_stats(f, h):
                dve.wait_ge(ff_read, TT * (f + 1) + 2 * h + 2)
                norm_stats("out", f, h, y_tile)
                add_eps("out", f, h)

            def norm_out_apply(f, h):
                norm_apply("out", f, h, y_tile, y_tile)

            def add_resid(f, h):
                for j in (2 * h, 2 * h + 1):
                    dve.wait_ge(normed["out"], TT * f + j + 1)
                    dve.tensor_tensor(y_tile(j), y_tile(j), col(resid, j, D),
                                      ALU.add).then_inc(out_set, 1)

            def keep_resid(f, a):
                if f is not None:
                    dve.wait_ge(out_set, TT * f + TT)
                dve.tensor_copy(resid[:, :], x_tok[:, :]).then_inc(resid_kept, 1)

            def split_dense():
                dve.wait_ge(dense_hi_set, 1)
                dve.tensor_tensor(dense_lo[:, :], dense_raw[:, :], dense_hi[:, :].bitcast(fp32),
                                  ALU.subtract).then_inc(dense_lo_set, 1)

            def body(f, a):
                n = 0

                def between(count):
                    nonlocal n
                    if f is None:
                        for _ in range(count):
                            round_piece(dve, DVE_PIECES[n], dve_rounded)
                            n += 1

                def h(layer, *tiles):
                    if f is not None:
                        for o in tiles:
                            hidden(f, layer, o)

                h(1, 0, 1)
                if a is None:
                    h(1, *range(2, HT))
                    h(2, *range(HT))
                    read_out(f, 0, 1)
                    norm_out_stats(f, 0)
                    read_out(f, 2)
                    norm_out_apply(f, 0)
                    read_out(f, 3)
                    norm_out_stats(f, 1)
                    add_resid(f, 0)
                    norm_out_apply(f, 1)
                    add_resid(f, 1)
                    return
                norm_x_stats(a)
                h(1, 2)
                norm_x_apply(a)
                if f is None:
                    split_dense()
                h(1, 3)
                for k in range(DT):
                    low(col(xT_lo, k), side[k][:, :], col(xT_hi, k), xT_hi_set,
                        DT * a + k + 1, xT_lo_set)
                between(1)
                h(1, 4)
                for e in range(DT):
                    low(col(qT_lo, e), side[2 + e][:, :], col(qT_hi, e), q_hi_set,
                        DT * a + e + 1, q_lo_set, scale=SCORE_SCALE)
                h(1, 5)
                for i in range(2):
                    low(col(v_lo, i), side[i][:, :], col(v_hi, i), v_hi_set, 2 * a + i + 1, v_lo_set)
                    between(1 - i)
                h(1, 6)
                row_maxima(a, 0)
                row_maxima(a, 1)
                h(1, 7)
                row_maxima(a, 2)
                row_maxima(a, 3)
                h(2, 0)
                probs_low(a, 0)
                probs_low(a, 1)
                h(2, 1)
                probs_low(a, 2)
                h(2, 2)
                between(1)
                probs_low(a, 3)
                norm_att_stats(a, 0)
                h(2, 3)
                norm_att_stats(a, 1)
                update_x(a, 0)
                h(2, 4)
                update_x(a, 1)
                norm_mid_apply(a, 0)
                h(2, 5)
                norm_mid_apply(a, 1)
                between(1)
                h(2, 6, 7)
                for k in range(DT):
                    low(col(fT_lo, k), side[k][:, :], col(fT_hi, k), fT_hi_set,
                        DT * a + k + 1, fT_lo_set)
                if f is not None:
                    read_out(f, *range(TT))
                between(1)
                if f is None:
                    for n_sum in DVE_SUMS:
                        wait_piece(dve, n_sum)
                        dve.tensor_reduce(low_sum[:, n_sum:n_sum + 1], low_halves(n_sum), AX.X,
                                          ALU.add).then_inc(dve_summed, 1)
                for o in range(HT):
                    first_gated(a, o)
                    if o > 0:
                        first_low(a, o - 1)
                    if o in (0, 3):
                        between(1)
                    if f is not None:
                        if o == 1:
                            norm_out_stats(f, 0)
                        if o == 2:
                            norm_out_stats(f, 1)
                        if o == 4:
                            norm_out_apply(f, 0)
                        if o == 5:
                            norm_out_apply(f, 1)
                first_low(a, HT - 1)
                keep_resid(f, a)

            dve.wait_ge(const_set, 7)
            run(dve, body)

        @block.tensor
        def _(pe):
            def three_pass(dst, lhs, rhs, start, stop):
                pe.matmul(dst, lhs[0], rhs[0], start=start, stop=False)
                pe.matmul(dst, lhs[0], rhs[1], start=False, stop=False)
                return pe.matmul(dst, lhs[1], rhs[0], start=False, stop=stop)

            def by_float32(dst, activations, weights, lhs_is_weight, start, stop):
                activations = activations.bitcast(fp32)
                lhs, rhs = (weights, activations) if lhs_is_weight else (activations, weights)
                return pe.matmul(dst, lhs, rhs, start=start, stop=stop)

            def keep_clock_up(products):
                for _ in range(products):
                    pe.matmul(main[3][:, 0:P], ident[:, :], ident[:, :])

            def transposes(a, n, done):
                for h in range(2):
                    pe.wait_ge(normed[n], TT * a + 2 * h + 2)
                    for k in range(DT):
                        for j in (2 * h, 2 * h + 1):
                            last = pe.transpose(side[k][:, j * P:(j + 1) * P],
                                                n_tok[:, j * D + k * P:j * D + (k + 1) * P],
                                                ident[:, :])
                        if h == 1:
                            last.then_inc(done, 1)

            def pair(hi, lo, first, cols):
                return hi[:, first:first + cols], lo[:, first:first + cols]

            def queries(a):
                if isinstance(a, int):
                    pe.wait_ge(dense_lo_set, 1)
                pe.wait_ge(xT_lo_set, DT * a + DT)
                for e in range(DT):
                    for k in range(DT):
                        last = three_pass(side[2 + e][:, :], pair(dense_hi, dense_lo, k * D + e * P, P),
                                          pair(xT_hi, xT_lo, k * S, S), k == 0, k == DT - 1)
                    last.then_inc(q_psum, 1)

            def values(a):
                for t in range(TT):
                    for k in range(DT):
                        last = three_pass(side[t // 2][:, (t % 2) * D:(t % 2 + 1) * D],
                                          pair(xT_hi, xT_lo, k * S + t * P, P),
                                          pair(dense_hi, dense_lo, (DT + k) * D, D),
                                          k == 0, k == DT - 1)
                    if t % 2:
                        last.then_inc(v_psum, 1)

            def scores(a, j):
                if j == 0:
                    pe.wait_ge(q_lo_set, DT * a + DT)
                if j >= 2:
                    pe.wait_ge(v_lo_set, 2 * a + j - 1)
                for k in range(DT):
                    last = three_pass(side[(j + 2) % 4][:, 0:(j + 1) * P],
                                      pair(qT_hi, qT_lo, k * S + j * P, P),
                                      pair(xT_hi, xT_lo, k * S, (j + 1) * P), k == 0, k == DT - 1)
                last.then_inc(scores_psum, 1)

            def probs_transposed(a, j):
                pe.wait_ge(probs_set, TT * a + j + 1)
                for t in range(j + 1):
                    last = pe.transpose(side[(j + 2) % 4][:, t * P:(t + 1) * P],
                                        probs[:, TRI[j] + t * P:TRI[j] + (t + 1) * P], ident[:, :])
                last.then_inc(pT_psum, 1)

            def attend(a, j):
                pe.wait_ge(pT_lo_set, TT * a + j + 1)
                for t in range(j + 1):
                    last = three_pass(side[2 + j // 2][:, (j % 2) * D:(j % 2 + 1) * D],
                                      pair(pT_hi, pT_lo, TRI[j] + t * P, P),
                                      pair(v_hi, v_lo, t * D, D), t == 0, t == j)
                if j % 2:
                    last.then_inc(att_psum, 1)

            def first_layer(f, o, full):
                if full:
                    pe.wait_ge(w_tile_loaded[0], 32 * (HT * f + o + 1))
                for part, name, done in ((0, "w1", gate_psum), (1, "w2", lin_psum)):
                    if o >= 2:
                        pe.wait_ge((gate_read, lin_read)[part], HT * f + o - 1)
                    for k in range(DT):
                        for src in (fT_hi, fT_lo):
                            dst, start, stop = (main[2 * (o % 2) + part][:, :],
                                                k == 0 and src is fT_hi, k == DT - 1 and src is fT_lo)
                            if full:
                                last = by_float32(dst, col(src, k), col(n_tok, part * DT + k, P),
                                                      True, start, stop)
                            else:
                                last = pe.matmul(dst, w_tile(name, k, o * P, P), col(src, k),
                                                 start=start, stop=stop)
                    last.then_inc(done, 1)

            def hidden(f, n, o, full):
                if o >= 4:
                    pe.wait_ge(gelu_set[n], HT * f + o - 3)
                elif n == 2:
                    pe.wait_ge(gelu_set[1], HT * f + o + 5)
                else:
                    pe.wait_ge((gate_read, lin_read)[o % 2], HT * f + HT - 1 + o // 2)
                if full:
                    pe.wait_ge(w_tile_loaded[n], 16 * (HT * f + o + 1))
                for k in range(HT):
                    for src, ready in ((hid_hi, hi_set), (hid_lo, lo_set)):
                        if o == 0:
                            pe.wait_ge(ready[n - 1], HT * f + k + 1)
                        start, stop = k == 0 and src is hid_hi, k == HT - 1 and src is hid_lo
                        x = col(src[(n - 1) % 2], k)
                        if full:
                            last = by_float32(main[o % 4][:, :], x, col(y_tok, k, P), True,
                                                  start, stop)
                        else:
                            last = pe.matmul(main[o % 4][:, :], w_tile(f"h{n}", k, o * P, P), x,
                                             start=start, stop=stop)
                last.then_inc(hid_psum[n], 1)

            def last_layer(f, j, full):
                if j >= 2:
                    pe.wait_ge(gelu_set[2], HT * f + HT - 3 + j)
                for k in range(HT):
                    if full and k % (HT // 2) == 0:
                        pe.wait_ge(w_tile_loaded[3], 16 * (HT * f + 2 * j + k // (HT // 2) + 1))
                    for src, ready in ((hid_hi, hi_set), (hid_lo, lo_set)):
                        if j == 0:
                            pe.wait_ge(ready[2], HT * f + k + 1)
                        dst = out_bank[j][:, 0:D]
                        start, stop = k == 0 and src is hid_hi, k == HT - 1 and src is hid_lo
                        x = src[0][:, k * S + j * P:k * S + (j + 1) * P]
                        if full:
                            last = by_float32(dst, x, col(n_tok, k % (HT // 2), D), False,
                                                  start, stop)
                        else:
                            last = pe.matmul(dst, x, w_tile("w3", k, 0, D), start=start, stop=stop)
                    if full and k == HT // 2 - 1:
                        last.then_inc(w3_half_used, 1)
                last.then_inc(ff_psum, 1)

            def either(flag, pieces):
                with pe.If_eq(flag, 0):
                    pieces(False)
                with pe.Else():
                    pieces(True)

            flags = [pe.alloc_register(f"pe_low_{g}") for g in range(len(LAYERS))]

            def sum_low_sums(stage):
                for g in FLAG_STAGES[stage]:
                    mine = [n for n, piece in enumerate(pieces) if piece[0] in LAYERS[g]]
                    wait_summed(pe, mine[-1] + 1)
                    for n in mine:
                        last = pe.matmul(flag_psum[stage][0:1, g:g + 1], ones[:, :],
                                         low_sum[:, n:n + 1], start=n == mine[0], stop=n == mine[-1])
                last.then_inc(low_sum_psum, 1)

            def body(f, a):
                def layer_0(full):
                    for o in range(HT):
                        if o == 1:
                            pe.wait_ge(ff_read, TT * a + TT)
                        first_layer(a, o, full)
                        if f is None and o == LAST_SUMS:
                            sum_low_sums(1)

                def layer_1(full):
                    def h(*tiles):
                        if f is not None:
                            for o in tiles:
                                hidden(f, 1, o, full)

                    h(0, 1, 2, 3)
                    if a is None:
                        h(4, 5, 6, 7)
                        return
                    transposes(a, "x", xT_psum)
                    if f is None:
                        keep_clock_up(8)
                    h(4)
                    queries(a)
                    h(5)
                    values(a)
                    h(6)
                    scores(a, 0)
                    scores(a, 1)
                    h(7)
                    scores(a, 2)
                    scores(a, 3)

                def layer_2(full):
                    def h(*tiles):
                        if f is not None:
                            for o in tiles:
                                hidden(f, 2, o, full)

                    h(0)
                    if a is None:
                        h(*range(1, HT))
                        return
                    probs_transposed(a, 0)
                    probs_transposed(a, 1)
                    h(1)
                    probs_transposed(a, 2)
                    attend(a, 0)
                    attend(a, 1)
                    h(2)
                    probs_transposed(a, 3)
                    h(3)
                    attend(a, 2)
                    attend(a, 3)
                    h(*range(4, HT))

                def layer_3(full):
                    for j in range(TT):
                        last_layer(f, j, full)

                if f is None:
                    layer_1(False)
                    layer_2(False)
                    sum_low_sums(0)
                    read_flags(pe, flags, 0)
                    pe.wait_ge(normed["att"], TT * a + 3)
                    keep_clock_up(10)
                    transposes(a, "mid", fT_psum)
                    keep_clock_up(8)
                    wait_rounded(pe, EARLY)
                else:
                    either(flags[1], layer_1)
                    either(flags[2], layer_2)
                    if a is not None:
                        transposes(a, "mid", fT_psum)
                    either(flags[3], layer_3)
                if a is not None:
                    pe.wait_ge(fT_lo_set, DT * a + DT)
                    either(flags[0], layer_0)
                if f is None:
                    read_flags(pe, flags, 1)
                    wait_rounded(pe, len(pieces))

            pe.wait_ge(const_set, 7)
            keep_clock_up(14)
            run(pe, body)


def kernel(L0_attn_input_data, L0_attn_qk, L0_attn_ov, L0_ffn_w1_w, L0_ffn_w1_s, L0_ffn_w2_w,
           L0_ffn_w2_s, L0_ffn_h1_w, L0_ffn_h1_s, L0_ffn_h2_w, L0_ffn_h2_s, L0_ffn_w3_w,
           L0_ffn_w3_s):
    import numpy as np
    import concourse.bacc as bacc
    from concourse.bass_utils import run_bass_kernel_spmd

    def rows(w):
        w = np.asarray(w)
        return np.ascontiguousarray(w.reshape(-1, P, w.shape[1]).transpose(1, 0, 2)).reshape(P, -1)

    def per_feature(s):
        return np.asarray(s).reshape(-1, P).T

    arrays = {
        "x": np.ascontiguousarray(L0_attn_input_data),
        "qk": rows(L0_attn_qk),
        "ov": rows(L0_attn_ov),
        "w1": rows(np.asarray(L0_ffn_w1_w).T),
        "w2": rows(np.asarray(L0_ffn_w2_w).T),
        "h1": rows(np.asarray(L0_ffn_h1_w).T),
        "h2": rows(np.asarray(L0_ffn_h2_w).T),
        "w3": rows(np.asarray(L0_ffn_w3_w).T),
        "scales": np.ascontiguousarray(np.concatenate(
            [per_feature(s) for s in (L0_ffn_w1_s, L0_ffn_w2_s, L0_ffn_h1_s, L0_ffn_h2_s)], axis=1)),
        "w3_scale": np.ascontiguousarray(L0_ffn_w3_s),
    }
    nc = bacc.Bacc("TRN2", target_bir_lowering=False, num_devices=1)
    args = [nc.dram_tensor(f"in_{n}", a.shape, mybir.dt.from_np(a.dtype), kind="ExternalInput").ap()
            for n, a in arrays.items()]
    shape = arrays["x"].shape
    out = nc.dram_tensor("out", shape, mybir.dt.float32, kind="ExternalOutput").ap()
    sandwich_kernel(nc, *args, out)
    r = run_bass_kernel_spmd(nc, [{f"in_{n}": a for n, a in arrays.items()}], core_ids=[0])
    return r.results[0]["out"]
```
